# Optimizing a Trainium2 kernel written in Bass

```python
import numpy as np
import jax
import jax.numpy as jnp

def _softmax(x, axis=-1):
    return jax.nn.softmax(x, axis=axis)

def _gelu(x):
    return jax.nn.gelu(x, approximate=True)

def _silu(x):
    return jax.nn.silu(x)

def _sigmoid(x):
    return jax.nn.sigmoid(x)

def _layernorm(x, axis=-1, eps=1e-05):
    m = jnp.mean(x, axis=axis, keepdims=True)
    v = jnp.var(x, axis=axis, keepdims=True)
    return (x - m) / jnp.sqrt(v + eps)

def _scatter_add(tgt, idx, src, axis=0):
    return tgt.at[idx].add(src)

def _segment_sum(src, seg, n):
    return jax.ops.segment_sum(src, seg, n)
kernel_name = 'mk_adaln_d1_jaxref_r8_7d505d'

def setup_inputs(seed: int=0):
    np.random.seed(seed)
    _w = jnp.asarray

    def _L0_attn_setup():
        import jax, jax.numpy as jnp
        import numpy as np
        BATCH = 2
        SEQLEN = 512
        D_MODEL = 128
        EXPAND = 2
        D_STATE = 128
        HEADDIM = 64
        D_CONV = 4
        NGROUPS = 1
        D_INNER = EXPAND * D_MODEL
        NHEADS = D_INNER // HEADDIM
        CONV_DIM = D_INNER + 2 * NGROUPS * D_STATE
        D_IN_PROJ = 2 * D_INNER + 2 * NGROUPS * D_STATE + NHEADS
        EPS = 1e-05

        def _mamba2_forward(X, W_in, conv_w, conv_b, dt_bias, A_log, D, norm_w, W_out):
            b, l, _ = X.shape
            zxbcdt = jnp.einsum('bld,ed->ble', X, W_in)
            z = zxbcdt[..., :D_INNER]
            xBC = zxbcdt[..., D_INNER:D_INNER + CONV_DIM]
            dt = zxbcdt[..., D_INNER + CONV_DIM:]
            xBC_t = jnp.transpose(xBC, (0, 2, 1))
            conv = jax.lax.conv_general_dilated(xBC_t, conv_w[:, None, :], window_strides=(1,), padding=[(D_CONV - 1, 0)], feature_group_count=CONV_DIM, dimension_numbers=('NCH', 'OIH', 'NCH'))
            xBC = jax.nn.silu(jnp.transpose(conv + conv_b[None, :, None], (0, 2, 1)))
            x = xBC[..., :D_INNER].reshape(b, l, NHEADS, HEADDIM)
            Bm = xBC[..., D_INNER:D_INNER + D_STATE]
            Cm = xBC[..., D_INNER + D_STATE:]
            dt = jax.nn.softplus(dt + dt_bias)
            A = -jnp.exp(A_log)
            dA = jnp.exp(dt * A)

            def step(h, inp):
                dA_t, dtx_t, B_t, C_t = inp
                h = h * dA_t[:, :, None, None] + dtx_t[..., None] * B_t[:, None, None, :]
                y = jnp.einsum('bhpn,bn->bhp', h, C_t)
                return (h, y)
            dtx = dt[..., None] * x
            h0 = jnp.zeros((b, NHEADS, HEADDIM, D_STATE), X.dtype)
            xs = (jnp.transpose(dA, (1, 0, 2)), jnp.transpose(dtx, (1, 0, 2, 3)), jnp.transpose(Bm, (1, 0, 2)), jnp.transpose(Cm, (1, 0, 2)))
            _, ys = jax.lax.scan(step, h0, xs)
            y = jnp.transpose(ys, (1, 0, 2, 3)) + D[None, None, :, None] * x
            y = y.reshape(b, l, D_INNER)
            y = y * jax.nn.silu(z)
            y = y * jax.lax.rsqrt(jnp.mean(jnp.square(y), axis=-1, keepdims=True) + EPS) * norm_w
            return jnp.einsum('ble,de->bld', y, W_out)
        key = jax.random.key(seed)
        ks = jax.random.split(key, 8)
        s = 0.02
        return {'X': jax.random.normal(ks[0], (BATCH, SEQLEN, D_MODEL), jnp.float32), 'W_in': jax.random.normal(ks[1], (D_IN_PROJ, D_MODEL), jnp.float32) * s, 'conv_w': jax.random.normal(ks[2], (CONV_DIM, D_CONV), jnp.float32) * 0.2, 'conv_b': jnp.zeros((CONV_DIM,), jnp.float32), 'dt_bias': jax.random.uniform(ks[3], (NHEADS,), jnp.float32) * 0.1, 'A_log': jnp.log(jax.random.uniform(ks[4], (NHEADS,), jnp.float32, minval=1.0, maxval=16.0)), 'D': jnp.ones((NHEADS,), jnp.float32), 'norm_w': jnp.ones((D_INNER,), jnp.float32), 'W_out': jax.random.normal(ks[5], (D_MODEL, D_INNER), jnp.float32) * s}
    _L0_attn_in = _L0_attn_setup()

    def _L0_ffn_setup():
        import jax, jax.numpy as jnp
        import numpy as np
        B, S, H, DFF, E, K = (2, 256, 128, 256, 8, 2)

        def _moe(x, Wg, W1, b1, W2, b2, W3, b3):
            Bm, Sm, Hm = x.shape
            xt = x.reshape(-1, Hm)
            gout = xt @ Wg.T
            topv, topi = jax.lax.top_k(gout, K)
            w = jax.nn.softmax(topv, axis=-1)
            comb = jnp.einsum('tke,tk->te', jax.nn.one_hot(topi, E, dtype=x.dtype), w)
            g = jnp.einsum('th,efh->etf', xt, W1) + b1[:, None, :]
            v = jnp.einsum('th,efh->etf', xt, W2) + b2[:, None, :]
            h = jax.nn.silu(g) * v
            eo = jnp.einsum('etf,ehf->eth', h, W3) + b3[:, None, :]
            out = jnp.einsum('eth,te->th', eo, comb)
            return out.reshape(Bm, Sm, Hm)
        key = jax.random.key(seed)
        ks = jax.random.split(key, 8)
        sc_h = 1.0 / np.sqrt(H)
        sc_f = 1.0 / np.sqrt(DFF)
        x = jax.random.normal(ks[0], (B, S, H), dtype=jnp.float32)
        Wg = jax.random.uniform(ks[1], (E, H), jnp.float32, -sc_h, sc_h)
        W1 = jax.random.uniform(ks[2], (E, DFF, H), jnp.float32, -sc_h, sc_h)
        b1 = jax.random.uniform(ks[3], (E, DFF), jnp.float32, -sc_h, sc_h)
        W2 = jax.random.uniform(ks[4], (E, DFF, H), jnp.float32, -sc_h, sc_h)
        b2 = jax.random.uniform(ks[5], (E, DFF), jnp.float32, -sc_h, sc_h)
        W3 = jax.random.uniform(ks[6], (E, H, DFF), jnp.float32, -sc_f, sc_f)
        b3 = jax.random.uniform(ks[7], (E, H), jnp.float32, -sc_f, sc_f)
        return {'x': x, 'Wg': Wg, 'W1': W1, 'b1': b1, 'W2': W2, 'b2': b2, 'W3': W3, 'b3': b3}
    _L0_ffn_in = _L0_ffn_setup()
    _L0_c = _w((lambda *s: np.random.randn(*s).astype(np.float32) * 0.05)(16, 128))
    _L0_wmod = _w((lambda *s: np.random.randn(*s).astype(np.float32) * 0.05)(128, 6 * 128) * 128 ** (-0.5))
    _d = {'L0_attn_X': _L0_attn_in['X'], 'L0_attn_W_in': _L0_attn_in['W_in'], 'L0_attn_conv_w': _L0_attn_in['conv_w'], 'L0_attn_conv_b': _L0_attn_in['conv_b'], 'L0_attn_dt_bias': _L0_attn_in['dt_bias'], 'L0_attn_A_log': _L0_attn_in['A_log'], 'L0_attn_D': _L0_attn_in['D'], 'L0_attn_norm_w': _L0_attn_in['norm_w'], 'L0_attn_W_out': _L0_attn_in['W_out'], 'L0_ffn_Wg': _L0_ffn_in['Wg'], 'L0_ffn_W1': _L0_ffn_in['W1'], 'L0_ffn_b1': _L0_ffn_in['b1'], 'L0_ffn_W2': _L0_ffn_in['W2'], 'L0_ffn_b2': _L0_ffn_in['b2'], 'L0_ffn_W3': _L0_ffn_in['W3'], 'L0_ffn_b3': _L0_ffn_in['b3'], 'L0_c': _L0_c, 'L0_wmod': _L0_wmod}
    _x0 = _d['L0_attn_X']
    _d['L0_attn_X'] = jax.random.normal(jax.random.fold_in(jax.random.key(seed), 1), (16, 512, 128), dtype=_x0.dtype)
    del _x0
    return _d

def reference(L0_attn_X, L0_attn_W_in, L0_attn_conv_w, L0_attn_conv_b, L0_attn_dt_bias, L0_attn_A_log, L0_attn_D, L0_attn_norm_w, L0_attn_W_out, L0_ffn_Wg, L0_ffn_W1, L0_ffn_b1, L0_ffn_W2, L0_ffn_b2, L0_ffn_W3, L0_ffn_b3, L0_c, L0_wmod):

    def _L0_attn_ref(X, W_in, conv_w, conv_b, dt_bias, A_log, D, norm_w, W_out):
        import jax, jax.numpy as jnp
        import numpy as np
        BATCH = 2
        SEQLEN = 512
        D_MODEL = 128
        EXPAND = 2
        D_STATE = 128
        HEADDIM = 64
        D_CONV = 4
        NGROUPS = 1
        D_INNER = EXPAND * D_MODEL
        NHEADS = D_INNER // HEADDIM
        CONV_DIM = D_INNER + 2 * NGROUPS * D_STATE
        D_IN_PROJ = 2 * D_INNER + 2 * NGROUPS * D_STATE + NHEADS
        EPS = 1e-05

        def _mamba2_forward(X, W_in, conv_w, conv_b, dt_bias, A_log, D, norm_w, W_out):
            b, l, _ = X.shape
            zxbcdt = jnp.einsum('bld,ed->ble', X, W_in)
            z = zxbcdt[..., :D_INNER]
            xBC = zxbcdt[..., D_INNER:D_INNER + CONV_DIM]
            dt = zxbcdt[..., D_INNER + CONV_DIM:]
            xBC_t = jnp.transpose(xBC, (0, 2, 1))
            conv = jax.lax.conv_general_dilated(xBC_t, conv_w[:, None, :], window_strides=(1,), padding=[(D_CONV - 1, 0)], feature_group_count=CONV_DIM, dimension_numbers=('NCH', 'OIH', 'NCH'))
            xBC = jax.nn.silu(jnp.transpose(conv + conv_b[None, :, None], (0, 2, 1)))
            x = xBC[..., :D_INNER].reshape(b, l, NHEADS, HEADDIM)
            Bm = xBC[..., D_INNER:D_INNER + D_STATE]
            Cm = xBC[..., D_INNER + D_STATE:]
            dt = jax.nn.softplus(dt + dt_bias)
            A = -jnp.exp(A_log)
            dA = jnp.exp(dt * A)

            def step(h, inp):
                dA_t, dtx_t, B_t, C_t = inp
                h = h * dA_t[:, :, None, None] + dtx_t[..., None] * B_t[:, None, None, :]
                y = jnp.einsum('bhpn,bn->bhp', h, C_t)
                return (h, y)
            dtx = dt[..., None] * x
            h0 = jnp.zeros((b, NHEADS, HEADDIM, D_STATE), X.dtype)
            xs = (jnp.transpose(dA, (1, 0, 2)), jnp.transpose(dtx, (1, 0, 2, 3)), jnp.transpose(Bm, (1, 0, 2)), jnp.transpose(Cm, (1, 0, 2)))
            _, ys = jax.lax.scan(step, h0, xs)
            y = jnp.transpose(ys, (1, 0, 2, 3)) + D[None, None, :, None] * x
            y = y.reshape(b, l, D_INNER)
            y = y * jax.nn.silu(z)
            y = y * jax.lax.rsqrt(jnp.mean(jnp.square(y), axis=-1, keepdims=True) + EPS) * norm_w
            return jnp.einsum('ble,de->bld', y, W_out)
        return _mamba2_forward(X, W_in, conv_w, conv_b, dt_bias, A_log, D, norm_w, W_out)

    def _L0_ffn_ref(x, Wg, W1, b1, W2, b2, W3, b3):
        import jax, jax.numpy as jnp
        import numpy as np
        B, S, H, DFF, E, K = (2, 256, 128, 256, 8, 2)

        def _moe(x, Wg, W1, b1, W2, b2, W3, b3):
            Bm, Sm, Hm = x.shape
            xt = x.reshape(-1, Hm)
            gout = xt @ Wg.T
            topv, topi = jax.lax.top_k(gout, K)
            w = jax.nn.softmax(topv, axis=-1)
            comb = jnp.einsum('tke,tk->te', jax.nn.one_hot(topi, E, dtype=x.dtype), w)
            g = jnp.einsum('th,efh->etf', xt, W1) + b1[:, None, :]
            v = jnp.einsum('th,efh->etf', xt, W2) + b2[:, None, :]
            h = jax.nn.silu(g) * v
            eo = jnp.einsum('etf,ehf->eth', h, W3) + b3[:, None, :]
            out = jnp.einsum('eth,te->th', eo, comb)
            return out.reshape(Bm, Sm, Hm)
        return _moe(x, Wg, W1, b1, W2, b2, W3, b3)
    x = L0_attn_X
    mod = (_silu(L0_c) @ L0_wmod).reshape(L0_c.shape[0], 6, 1, -1)
    sa, ca, ga, sb, cb, gb = (mod[:, 0], mod[:, 1], mod[:, 2], mod[:, 3], mod[:, 4], mod[:, 5])
    ga = (2 * (ga >= 0) - 1) * jnp.maximum(jnp.abs(ga), 0.25)
    gb = (2 * (gb >= 0) - 1) * jnp.maximum(jnp.abs(gb), 0.25)
    h = _layernorm(x, axis=-1) * (1 + ca) + sa
    x = x + ga * _L0_attn_ref(h, L0_attn_W_in, L0_attn_conv_w, L0_attn_conv_b, L0_attn_dt_bias, L0_attn_A_log, L0_attn_D, L0_attn_norm_w, L0_attn_W_out)
    h = _layernorm(x, axis=-1) * (1 + cb) + sb
    x = x + gb * _L0_ffn_ref(h, L0_ffn_Wg, L0_ffn_W1, L0_ffn_b1, L0_ffn_W2, L0_ffn_b2, L0_ffn_W3, L0_ffn_b3)
    return x

_drawn_inputs = setup_inputs


def setup_inputs(seed=0):
    import zlib

    import numpy as np

    out = dict(_drawn_inputs(seed))
    spreads = {'L0_attn_conv_b': (0.0, 0.1), 'L0_attn_D': (1.0, 0.6), 'L0_attn_norm_w': (1.0, 0.6)}
    factors = {'L0_attn_dt_bias': 45.532,
     'L0_attn_A_log': 8.0,
     'L0_ffn_Wg': 3.195,
     'L0_ffn_W1': 3.07,
     'L0_ffn_b1': 8.0,
     'L0_ffn_W2': 2.99,
     'L0_ffn_b2': 8.0,
     'L0_ffn_W3': 2.973,
     'L0_ffn_b3': 8.0}
    for name, (base, spread) in spreads.items():
        noise = np.random.default_rng([zlib.crc32(name.encode()), seed]).standard_normal(out[name].shape)
        drawn = base * np.exp(spread * noise) if base else spread * noise
        out[name] = jnp.asarray(drawn.astype(out[name].dtype))
    for name, factor in factors.items():
        out[name] = (out[name] * factor).astype(out[name].dtype)
    return out
```

```python
from contextlib import ExitStack

import concourse.bass as bass
from concourse import mybir

ALU = mybir.AluOpType
ACT = mybir.ActivationFunctionType
F32 = mybir.dt.float32
F32R = mybir.dt.float32r
U32 = mybir.dt.uint32

P = 128
B = 16
L = 512
C = L // P
D = 128
DI = 256
NH = 4
HD = DI // NH
NCT = 4
KC = 4
E = 8
FT = 2
U = E * FT
EPS = 1e-5
SA, CA, GA, SB, CB, GB = range(6)


def program(nc, d):
    ctx = ExitStack()
    with ctx:
        def sb(name, shape, dt=F32):
            return ctx.enter_context(nc.sbuf_tensor(name, shape, dt))

        def bank(name):
            return ctx.enter_context(nc.psum_tensor(name, [P, 512], F32))

        def sem(name):
            return ctx.enter_context(nc.semaphore(name))

        ident = sb("ident", [P, P])
        upto = sb("upto", [P, P])
        upto_r = sb("upto_r", [P, P], F32R)
        after = sb("after", [P, P])
        after_r = sb("after_r", [P, P], F32R)
        ones_r = sb("ones_r", [P, P], F32R)
        expo = sb("expo", [P, C])
        experts = sb("experts", [P, E])
        win = sb("win", [P, 772])
        win_hi = sb("win_hi", [P, 772], F32R)
        win_lo = sb("win_lo", [P, 772], F32R)
        w12 = sb("w12", [P, 2 * U * P])
        w12_hi = sb("w12_hi", [P, 2 * U * P], F32R)
        w12_lo = sb("w12_lo", [P, 2 * U * P], F32R)
        w3 = sb("w3", [P, U, D])
        wout = sb("wout", [P, 2, D])
        woutn = sb("woutn", [P, 2, D])
        wg = sb("wg", [P, E])
        cols = sb("cols", [P, NCT * (KC + 1) + 2 * U + 2])
        rows = sb("rows", [P, NH * 3 * C + DI])
        b3 = sb("b3", [E, D])
        wmod = sb("wmod", [P, 6, D])
        ct = sb("ct", [P, B])
        cs = sb("cs", [P, B])
        mod = sb("mod", [P, 6, B])
        nega = sb("nega", [P, C * NH])

        conv_w = cols[:, 0:NCT * KC]
        conv_b = cols[:, NCT * KC:NCT * (KC + 1)]
        b12 = cols[:, NCT * (KC + 1):NCT * (KC + 1) + 2 * U]
        norm_w = cols[:, NCT * (KC + 1) + 2 * U:]
        dt_bias = rows[:, 0:C * NH]
        a_log = rows[:, C * NH:2 * C * NH]
        d_row = rows[:, 3 * C * NH:3 * C * NH + DI]

        x = sb("x", [P, 2, C, D])
        touch = sb("touch", [P, 2 + C])
        stats = sb("stats", [P, C, 6])
        mv = sb("mv", [P, C, 2])
        var = sb("var", [P, C])
        rstd = sb("rstd", [P, C])
        xn = sb("xn", [P, C, D])
        h = sb("h", [P, L])
        h_hi = sb("h_hi", [P, L], F32R)
        h_lo = sb("h_lo", [P, L], F32R)
        ccol = sb("ccol", [P, P])
        gabs = sb("gabs", [P, 2 * D])
        gsign = sb("gsign", [P, 2 * D])
        gate = sb("gate", [P, 2, 2 * D])
        wo = sb("wo", [P, 2, D])
        sp = [sb(f"sp{i}", [P, C * NH]) for i in range(10)]
        dt = sb("dt", [P, C * NH])
        da = sb("da", [P, C * NH])
        da_hi = sb("da_hi", [P, C * NH], F32R)
        da_lo = sb("da_lo", [P, C * NH], F32R)
        mda_hi = sb("mda_hi", [P, 2, NH, P], F32R)
        mda_lo = sb("mda_lo", [P, 2, NH, P], F32R)
        decay = sb("decay", [P, C, NH, P])
        edge = sb("edge", [P, C, 2, NH])
        xbc = sb("xbc", [P, NCT, L])
        zs = sb("zs", [P, C, DI])
        tok = sb("tok", [P, C, DI + P])
        xdt = sb("xdt", [P, C, DI])
        xdecay = sb("xdecay", [P, C, DI])
        xskip = sb("xskip", [P, C, DI])
        gm = sb("gm", [P, C, P])
        mix = sb("mix", [P, C, NH, P])
        state = sb("state", [P, C - 1, DI])
        faded = sb("faded", [P, C - 1, DI])
        ysum = sb("ysum", [P, C, DI])
        y = sb("y", [P, C, DI])
        ss = sb("ss", [P, C])
        ms = sb("ms", [P, C])
        rstdy = sb("rstdy", [P, C])
        yt = sb("yt", [P, C, 2, P])
        x1 = sb("x1", [P, 2, C, D])
        h2 = sb("h2", [P, L])
        h2_hi = sb("h2_hi", [P, 2, L], F32R)
        h2_lo = sb("h2_lo", [P, 2, L], F32R)
        logit = sb("logit", [P, C, E])
        top = sb("top", [P, C, E])
        topi = sb("topi", [P, C, E], U32)
        topf = sb("topf", [P, C, 2])
        gap = sb("gap", [P, C])
        tanh = sb("tanh", [P, C])
        wtop = sb("wtop", [P, C, 2])
        pick = sb("pick", [P, C, E])
        comb = sb("comb", [P, 2, C, E])
        combt = sb("combt", [E, L])
        sg = sb("sg", [P, 2, L])
        hid = sb("hid", [P, 2, FT, L])
        acc = sb("acc", [P, 2, C, D])
        xo = sb("xo", [P, 2, C, D])

        m0, m1, m2 = bank("m0"), bank("m1"), bank("m2")
        pg = [bank("pg0"), bank("pg1")]
        pv = [bank("pv0"), bank("pv1")]
        po = bank("po")

        consts_in, win_in, w12_in, w3_in = sem("consts_in"), sem("win_in"), sem("w12_in"), sem("w3_in")
        s_vec, s_act = sem("setup_vector_step"), sem("setup_scalar_step")
        s_cs, s_mod, s_modt = sem("silu_c_ready"), sem("mod_psum"), sem("mod_ready")
        w12_ready = sem("w12_split")
        const_ready = sem("constants_ready")
        pool_const = sem("pool_constants")
        x_in, x_out = sem("x_loaded"), sem("x_stored")
        acc_started = sem("acc_started")
        vs = sem("vector_step")
        gcol = sem("gate_column")
        gate_psum, gate_taken, wo_ready = sem("gate_psum"), sem("gate_taken"), sem("wo_ready")
        var1, rstd1, xn1, ht_psum = sem("var1"), sem("rstd1"), sem("xn1"), sem("ht_psum")
        h_ready, hhi_ready, hlo_ready = sem("h_ready"), sem("hhi_ready"), sem("hlo_ready")
        dt_psum, dt_taken = sem("dt_psum"), sem("dt_taken")
        sp_neg, sp_exp, sp_w, sp_ln, da_ready = sem("sp_neg"), sem("sp_exp"), sem("sp_w"), sem("sp_ln"), sem("da_ready")
        in_psum, tap0, tapped, silued = sem("in_psum"), sem("tap0"), sem("tapped"), sem("silued")
        z_psum, z_ready = sem("z_psum"), sem("z_ready")
        mda_ready, seg_psum, decayed = sem("mda_ready"), sem("seg_psum"), sem("decayed")
        edge_psum, edge_ready = sem("edge_psum"), sem("edge_ready")
        g_psum, gm_ready, mixed = sem("g_psum"), sem("gm_ready"), sem("mixed")
        tok_psum, tok_ready = sem("tok_psum"), sem("tok_ready")
        xdt_ready, xdecay_ready, xskip_ready = sem("xdt_ready"), sem("xdecay_ready"), sem("xskip_ready")
        snew_psum, state_ready = sem("snew_psum"), sem("state_ready")
        y_psum, y_taken, y_ready, sq_ready = sem("y_psum"), sem("y_taken"), sem("y_ready"), sem("sq_ready")
        yt_psum, yt_ready, out_psum = sem("yt_psum"), sem("yt_ready"), sem("out_psum")
        ms_ready, rstdy_ready, x1_ready = sem("ms_ready"), sem("rstdy_ready"), sem("x1_ready")
        var2, rstd2, xn2, h2t_psum = sem("var2"), sem("rstd2"), sem("xn2"), sem("h2t_psum")
        h2_ready, h2hi_ready, h2lo_ready = sem("h2_ready"), sem("h2hi_ready"), sem("h2lo_ready")
        route_psum, gap_ready, tanh_ready = sem("route_psum"), sem("gap_ready"), sem("tanh_ready")
        comb_ready, combt_psum, combt_ready, b3_psum = sem("comb_ready"), sem("combt_psum"), sem("combt_ready"), sem("b3_psum")
        eg_psum, ev_psum, sg_ready, hid_ready = sem("eg_psum"), sem("ev_psum"), sem("sg_ready"), sem("hid_ready")
        o_psum, acc_ready = sem("o_psum"), sem("acc_ready")
        gated_ready, xo_ready = sem("gated_ready"), sem("xo_ready")

        def wait(eng, s, b, per, n=0):
            v = b * per + n
            if not isinstance(v, int) or v > 0:
                eng.wait_ge(s, v)

        def wide(ap, n):
            return ap.unsqueeze(2).to_broadcast([P, ap.shape[1], n])

        def run(eng, steps):
            steps(0, 0, None)
            steps(1, 1, 0)
            with eng.Fori(0, (B - 2) // 2) as j:
                for k in range(2):
                    steps(2 * j + 2 + k, k, 2 * j + 1 + k)
            steps(None, B % 2, B - 1)

        block = ctx.enter_context(nc.Block())

        @block.sync
        def _(sp_):
            for dst, src in ((ident, "ident"), (upto, "upto"), (after, "after"), (expo, "expo"), (experts, "experts"),
                             (cols, "cols"), (rows, "rows"), (wg, "wg"), (ct, "ct"), (b3, "b3")):
                sp_.dma_start(dst[:, :], d[src]).then_inc(consts_in, 16)
            sp_.dma_start(wout[:, :, :], d["wout"]).then_inc(consts_in, 16)
            sp_.dma_start(wmod[:, :, :], d["wmod"]).then_inc(consts_in, 16)
            xv = d["x"].rearrange("b (c p) m -> b p c m", p=P)
            ov = d["out"].rearrange("b (c p) m -> b p c m", p=P)
            sp_.dma_start(x[:, 0, :, :], xv[0]).then_inc(x_in, 16)
            sp_.wait_ge(x_in, 16)
            sp_.dma_start(x[:, 1, :, :], xv[1]).then_inc(x_in, 16)

            def steps(b, par, q):
                if b is not None and not (isinstance(b, int) and b < 2):
                    sp_.wait_ge(x1_ready, b - 1)
                    sp_.wait_ge(x_in, b * 16)
                    sp_.dma_start(x[:, par, :, :], xv[b]).then_inc(x_in, 16)
                if q is not None:
                    wait(sp_, x_out, q, 16)
                    wait(sp_, xo_ready, q, 1, 1)
                    sp_.dma_start(ov[q], xo[:, 1 - par, :, :]).then_inc(x_out, 16)

            run(sp_, steps)
            sp_.wait_ge(x_out, 16 * B)

        @block.gpsimd
        def _(pool):
            pool.dma_start(win[:, :], d["win"]).then_inc(win_in, 16)
            pool.dma_start(w12[:, :], d["w12"]).then_inc(w12_in, 16)
            pool.dma_start(w3[:, :, :], d["w3"]).then_inc(w3_in, 16)
            pool.wait_ge(consts_in, 16 * 12)
            pool.wait_ge(const_ready, 1)

            def power(dst, src, ready, b, done):
                wait(pool, ready, b, 1, 1)
                nc.gpsimd.tensor_tensor(out=dst[:, :], in0=src[:, :], in1=expo[:, :], op=ALU.pow).then_inc(done, 1)

            def steps(b, par, q):
                for u in range(U):
                    if b is not None:
                        if u == 0:
                            wait(pool, b3_psum, b, 1)
                            wait(pool, acc_started, b, 1)
                            wait(pool, comb_ready, b, 1)
                            power(rstd, var, var1, b, rstd1)
                        if u == 1:
                            wait(pool, hhi_ready, b, 1, 1)
                            nc.gpsimd.tensor_tensor(out=h_lo[:, :], in0=h[:, :], in1=h_hi[:, :].bitcast(F32),
                                                    op=ALU.subtract).then_inc(hlo_ready, 1)
                        if 4 <= u < 4 + C:
                            c = u - 4
                            if c == 0:
                                wait(pool, da_ready, b, 1, 1)
                            if c >= 2:
                                wait(pool, seg_psum, b, C, c - 1)
                            if c != 1:
                                nc.gpsimd.tensor_tensor(out=touch[:, 2 + c:3 + c], in0=expo[:, 0:1], in1=expo[:, 0:1], op=ALU.mult)
                            for n in range(NH):
                                k = c * NH + n
                                nc.gpsimd.tensor_scalar(mda_hi[:, c % 2, n, :], upto[:, :], da_hi[:, k:k + 1].bitcast(F32), 1.0,
                                                        ALU.mult, ALU.mult)
                                last = nc.gpsimd.tensor_scalar(mda_lo[:, c % 2, n, :], upto[:, :], da_lo[:, k:k + 1].bitcast(F32),
                                                               1.0, ALU.mult, ALU.mult)
                            last.then_inc(mda_ready, 1)
                        if 8 <= u < 8 + C:
                            c = u - 8
                            wait(pool, tok_ready, b, C, c + 1)
                            wait(pool, decayed, b, C, c + 1)
                            xt = tok[:, c, 0:DI].rearrange("p (h d) -> p h d", h=NH)
                            nc.gpsimd.tensor_tensor(out=xdt[:, c, :].rearrange("p (h d) -> p h d", h=NH), in0=xt,
                                                    in1=wide(dt[:, c * NH:(c + 1) * NH], HD), op=ALU.mult).then_inc(xdt_ready, 1)
                            if c < C - 1:
                                wait(pool, xdt_ready, b, C, c + 1)
                                nc.gpsimd.tensor_tensor(out=xdecay[:, c, :].rearrange("p (h d) -> p h d", h=NH),
                                                        in0=xdt[:, c, :].rearrange("p (h d) -> p h d", h=NH),
                                                        in1=wide(decay[:, c, :, P - 1], HD), op=ALU.mult).then_inc(xdecay_ready, 1)
                            nc.gpsimd.tensor_tensor(out=xskip[:, c, :], in0=tok[:, c, 0:DI], in1=d_row,
                                                    op=ALU.mult).then_inc(xskip_ready, 1)
                        if u == 13:
                            power(rstdy, ms, ms_ready, b, rstdy_ready)
                        if u == 14:
                            power(rstd, var, var2, b, rstd2)
                        if u == 15:
                            wait(pool, h2hi_ready, b, 1, 1)
                            nc.gpsimd.tensor_tensor(out=h2_lo[:, par, :], in0=h2[:, :], in1=h2_hi[:, par, :].bitcast(F32),
                                                    op=ALU.subtract).then_inc(h2lo_ready, 1)
                if q is not None:
                    p2 = 1 - par
                    wait(pool, acc_ready, q, E, E)
                    wait(pool, x_out, q, 16)
                    nc.gpsimd.tensor_tensor(out=xo[:, p2, :, :], in0=acc[:, p2, :, :],
                                            in1=gate[:, p2, D:2 * D].unsqueeze(1).to_broadcast([P, C, D]),
                                            op=ALU.mult).then_inc(gated_ready, 1)
                    wait(pool, gated_ready, q, 1, 1)
                    nc.gpsimd.tensor_tensor(out=xo[:, p2, :, :], in0=xo[:, p2, :, :], in1=x1[:, p2, :, :],
                                            op=ALU.add).then_inc(xo_ready, 1)

            run(pool, steps)

        @block.scalar
        def _(act):
            act.wait_ge(consts_in, 16 * 12)
            nc.scalar.activation(cs[:, :], ct[:, :], ACT.Silu).then_inc(s_cs, 1)
            act.wait_ge(s_mod, 1)
            for r in (SA, SB):
                nc.scalar.activation(mod[:, r, :], m0[:, r * B:(r + 1) * B], ACT.Copy)
            for r in (CA, CB):
                last = nc.scalar.activation(mod[:, r, :], m0[:, r * B:(r + 1) * B], ACT.Copy, bias=1.0)
            last.then_inc(s_modt, 1)
            nc.scalar.activation(sp[9][:, :], a_log, ACT.Exp).then_inc(s_act, 1)
            act.wait_ge(s_modt, 1)
            act.wait_ge(s_act, 1)

            def steps(b, par, q):
                def expert_silu(u):
                    wait(act, eg_psum, q, U, u + 1)
                    wait(act, hid_ready, q, U, max(u - 1, 0))
                    nc.scalar.activation(sg[:, u % 2, :], pg[u % 2][:, :], ACT.Silu,
                                         bias=b12[:, 2 * u:2 * u + 1]).then_inc(sg_ready, 1)

                def conv_first(i):
                    wait(act, in_psum, b, NCT, i + 1)
                    nc.scalar.activation(xbc[:, i, :], (m0, m1)[i % 2][:, :], ACT.Identity, bias=conv_b[:, i:i + 1],
                                         scale=conv_w[:, i * KC + KC - 1:i * KC + KC]).then_inc(tap0, 1)

                def conv_silu(i):
                    wait(act, tapped, b, NCT, i + 1)
                    nc.scalar.activation(xbc[:, i, :], xbc[:, i, :], ACT.Silu).then_inc(silued, 1)

                def z_silu(k):
                    wait(act, z_psum, b, 2, k + 1)
                    nc.scalar.activation(zs[:, 2 * k:2 * k + 2, :].rearrange("p c e -> p (c e)"), m2[:, :],
                                         ACT.Silu).then_inc(z_ready, 1)

                for u in range(U):
                    if q is not None:
                        expert_silu(u)
                    if b is None:
                        continue
                    if u == 0:
                        wait(act, b3_psum, b, 1)
                        wait(act, comb_ready, b, 1)
                        wait(act, h2lo_ready, b, 1)
                        nc.scalar.activation(ccol[:, :], cs[:, bass.ds(b, 1)].to_broadcast([P, P]), ACT.Copy).then_inc(gcol, 1)
                    if u == 1:
                        wait(act, ht_psum, b, 1, 1)
                        for dst, s in ((h, h_ready), (h_hi, hhi_ready)):
                            nc.scalar.activation(dst[:, :], m0[:, :], ACT.Identity, bias=mod[:, SA, bass.ds(b, 1)],
                                                 scale=mod[:, CA, bass.ds(b, 1)]).then_inc(s, 1)
                    if u == 2:
                        conv_first(0)
                        wait(act, sp_neg, b, 1, 1)
                        nc.scalar.activation(sp[2][:, :], sp[1][:, :], ACT.Exp).then_inc(sp_exp, 1)
                        wait(act, sp_w, b, 1, 1)
                        nc.scalar.activation(sp[4][:, :], sp[3][:, :], ACT.Ln).then_inc(sp_ln, 1)
                    if u == 3:
                        conv_first(1)
                        z_silu(0)
                    if u == 4:
                        conv_first(2)
                        conv_silu(0)
                        z_silu(1)
                    if u == 5:
                        conv_first(3)
                        conv_silu(1)
                    if u == 6:
                        conv_silu(2)
                        conv_silu(3)
                    if u == 7:
                        wait(act, edge_psum, b, 1, 1)
                        nc.scalar.activation(edge[:, :, :, :].rearrange("p c k h -> p (c k h)"), m1[:, 0:2 * C * NH],
                                             ACT.Exp).then_inc(edge_ready, 1)
                        for c in range(C):
                            wait(act, seg_psum, b, C, c + 1)
                            nc.scalar.activation(decay[:, c, :, :].rearrange("p h t -> p (h t)"), (m2, m0)[c % 2][:, :],
                                                 ACT.Exp).then_inc(decayed, 1)
                    for c in {8: (0, 1), 9: (2, 3)}.get(u, ()):
                        wait(act, tok_psum, b, C, c + 1)
                        nc.scalar.activation(tok[:, c, :], m0[:, 0:DI + P], ACT.Copy).then_inc(tok_ready, 1)
                    if 9 < u <= 9 + C:
                        c = u - 10
                        wait(act, yt_psum, b, C, c + 1)
                        nc.scalar.activation(yt[:, c, :, :].rearrange("p k t -> p (k t)"), m0[:, 0:DI],
                                             ACT.Copy).then_inc(yt_ready, 1)
                        wait(act, sq_ready, b, C, c)
                        nc.scalar.activation(ysum[:, c, :], y[:, c, :], ACT.Square, accum_out=ss[:, c:c + 1]).then_inc(sq_ready, 1)
                if b is not None:
                    wait(act, h2t_psum, b, 1, 1)
                    for dst, s in ((h2[:, :], h2_ready), (h2_hi[:, par, :], h2hi_ready)):
                        nc.scalar.activation(dst, m0[:, :], ACT.Identity, bias=mod[:, SB, bass.ds(b, 1)],
                                             scale=mod[:, CB, bass.ds(b, 1)]).then_inc(s, 1)
                    wait(act, gap_ready, b, 1, 1)
                    nc.scalar.activation(tanh[:, :], gap[:, :], ACT.Tanh, scale=0.5).then_inc(tanh_ready, 1)
                    wait(act, combt_psum, b, 1, 1)
                    nc.scalar.activation(combt[:, :], m1[0:E, :], ACT.Copy).then_inc(combt_ready, 1)
                    wait(act, b3_psum, b, 1, 1)
                    wait(act, xo_ready, b, 1, -1)
                    nc.scalar.activation(acc[:, par, :, :].rearrange("p c m -> p (c m)"), m2[:, :],
                                         ACT.Copy).then_inc(acc_started, 1)

            run(act, steps)

        @block.vector
        def _(vec):
            vec.wait_ge(win_in, 16)
            nc.vector.tensor_copy(win_hi[:, :], win[:, :]).then_inc(s_vec, 1)
            vec.wait_ge(s_vec, 1)
            nc.vector.tensor_tensor(out=win_lo[:, :], in0=win[:, :], in1=win_hi[:, :].bitcast(F32), op=ALU.subtract)
            vec.wait_ge(consts_in, 16 * 12)
            nc.vector.tensor_copy(upto_r[:, :], upto[:, :])
            nc.vector.tensor_copy(after_r[:, :], after[:, :])
            nc.vector.tensor_scalar(ones_r[:, :], upto[:, :], 0.0, 1.0, ALU.mult, ALU.add)
            for k in range(2):
                nc.vector.tensor_scalar(woutn[:, k, :], wout[:, k, :], norm_w[:, k:k + 1], None, ALU.mult)
            vec.wait_ge(s_act, 1)
            nc.vector.tensor_scalar(nega[:, :], sp[9][:, :], -1.0, None, ALU.mult).then_inc(const_ready, 1)
            vec.wait_ge(const_ready, 1)

            STEPS = 37

            def steps(b, par, q):
                count = [0]

                def link(ins):
                    count[0] += 1
                    ins.then_inc(vs, 1)
                    wait(vec, vs, b, STEPS, count[0])

                def norm(src, ready_var, ready_rstd, done):
                    for c in range(C):
                        last = nc.vector.bn_stats(stats[:, c, :], src[:, c, :])
                    link(last)
                    nc.vector.tensor_copy(touch[:, 0:1], stats[:, 0, 0:1])
                    for c in range(C):
                        last = nc.vector.bn_aggr(mv[:, c, :], stats[:, c, :])
                    link(last)
                    nc.vector.tensor_scalar(var[:, :], mv[:, :, 1], EPS, None, ALU.add).then_inc(ready_var, 1)
                    return mv

                def norm_end(src, ready_rstd, done):
                    wait(vec, ready_rstd, b, 1, 1)
                    for c in range(C):
                        last = nc.vector.tensor_scalar(xn[:, c, :], src[:, c, :], mv[:, c, 0:1], rstd[:, c:c + 1],
                                                       ALU.subtract, ALU.mult)
                    last.then_inc(done, 1)

                def conv_taps(i):
                    wait(vec, tap0, b, NCT, i + 1)
                    for k in range(1, KC):
                        w = conv_w[:, i * KC + KC - 1 - k:i * KC + KC - k]
                        last = nc.vector.scalar_tensor_tensor(out=xbc[:, i, k:L], in0=(m0, m1)[i % 2][:, 0:L - k], scalar=w,
                                                              in1=xbc[:, i, k:L], op0=ALU.mult, op1=ALU.add)
                        if k < KC - 1:
                            link(last)
                    last.then_inc(tapped, 1)

                def y_chunk(c):
                    wait(vec, y_psum, b, C, c + 1)
                    wait(vec, xskip_ready, b, C, c + 1)
                    if c == 0:
                        nc.vector.tensor_tensor(out=ysum[:, c, :], in0=m2[:, 0:DI], in1=xskip[:, c, :],
                                                op=ALU.add).then_inc(y_taken, 1)
                        wait(vec, y_taken, b, C, c + 1)
                    else:
                        link(nc.vector.tensor_tensor(out=ysum[:, c, :].rearrange("p (h d) -> p h d", h=NH),
                                                     in0=m2[:, DI:2 * DI].rearrange("p (h d) -> p h d", h=NH),
                                                     in1=wide(edge[:, c, 0, :], HD), op=ALU.mult))
                        nc.vector.tensor_tensor(out=ysum[:, c, :], in0=m2[:, 0:DI], in1=ysum[:, c, :],
                                                op=ALU.add).then_inc(y_taken, 1)
                        wait(vec, y_taken, b, C, c + 1)
                        link(nc.vector.tensor_tensor(out=ysum[:, c, :], in0=ysum[:, c, :], in1=xskip[:, c, :], op=ALU.add))
                    wait(vec, z_ready, b, 2, c // 2 + 1)
                    nc.vector.tensor_tensor(out=y[:, c, :], in0=ysum[:, c, :], in1=zs[:, c, :],
                                            op=ALU.mult).then_inc(y_ready, 1)

                def hidden(u):
                    e, f = u // FT, u % FT
                    wait(vec, sg_ready, q, U, u + 1)
                    wait(vec, ev_psum, q, U, u + 1)
                    if f == 0 and e >= 2:
                        wait(vec, o_psum, q, E, e - 1)
                    nc.vector.scalar_tensor_tensor(out=hid[:, e % 2, f, :], in0=pv[u % 2][:, :], scalar=b12[:, 2 * u + 1:2 * u + 2],
                                                   in1=sg[:, u % 2, :], op0=ALU.add, op1=ALU.mult).then_inc(hid_ready, 1)

                def accumulate(e):
                    p2 = 1 - par
                    wait(vec, o_psum, q, E, e + 1)
                    if e == 0:
                        wait(vec, acc_started, q, 1, 1)
                    wait(vec, acc_ready, q, E, e)
                    for c in range(C):
                        last = nc.vector.scalar_tensor_tensor(out=acc[:, p2, c, :], in0=po[:, c * D:(c + 1) * D],
                                                              scalar=comb[:, p2, c, e:e + 1], in1=acc[:, p2, c, :],
                                                              op0=ALU.mult, op1=ALU.add)
                    last.then_inc(acc_ready, 1)

                for u in range(U):
                    if q is not None:
                        hidden(u)
                        if u % 2 == 1 and u > 2:
                            accumulate(u // 2 - 1)
                    if b is None:
                        continue
                    if u == 0:
                        wait(vec, b3_psum, b, 1)
                        wait(vec, acc_started, b, 1)
                        wait(vec, h2lo_ready, b, 1)
                        wait(vec, x_in, b, 16, 16)
                        norm(x[:, par, :, :], var1, rstd1, xn1)
                        wait(vec, gate_psum, b, 1, 1)
                        link(nc.vector.tensor_scalar(gsign[:, :], m2[:, 0:2 * D], 0.0, 2.0, ALU.is_ge, ALU.mult))
                        nc.vector.scalar_tensor_tensor(out=gabs[:, :], in0=gsign[:, :], scalar=-1.0, in1=m2[:, 0:2 * D],
                                                       op0=ALU.add, op1=ALU.mult).then_inc(gate_taken, 1)
                        wait(vec, gate_taken, b, 1, 1)
                        link(nc.vector.tensor_scalar(gabs[:, :], gabs[:, :], 0.25, None, ALU.max))
                        wait(vec, xo_ready, b, 1, -1)
                        link(nc.vector.scalar_tensor_tensor(out=gate[:, par, :], in0=gsign[:, :], scalar=-1.0, in1=gabs[:, :],
                                                            op0=ALU.add, op1=ALU.mult))
                        nc.vector.tensor_tensor(out=wo[:, :, :], in0=woutn[:, :, :],
                                                in1=gate[:, par, 0:D].unsqueeze(1).to_broadcast([P, 2, D]),
                                                op=ALU.mult).then_inc(wo_ready, 1)
                        norm_end(x[:, par, :, :], rstd1, xn1)
                    if u == 2:
                        wait(vec, dt_psum, b, 1, 1)
                        nc.vector.tensor_tensor(out=sp[0][:, :], in0=m1[:, 0:C * NH], in1=dt_bias, op=ALU.add).then_inc(dt_taken, 1)
                        wait(vec, dt_taken, b, 1, 1)
                        nc.vector.scalar_tensor_tensor(out=sp[1][:, :], in0=sp[0][:, :], scalar=-1.0, in1=sp[0][:, :],
                                                       op0=ALU.mult, op1=ALU.min).then_inc(sp_neg, 1)
                        wait(vec, sp_exp, b, 1, 1)
                        nc.vector.tensor_scalar(sp[3][:, :], sp[2][:, :], 1.0, None, ALU.add).then_inc(sp_w, 1)
                        conv_taps(0)
                    if u == 3:
                        wait(vec, sp_w, b, 1, 1)
                        link(nc.vector.tensor_scalar(sp[5][:, :], sp[3][:, :], -1.0, 1e-30, ALU.add, ALU.max))
                        link(nc.vector.reciprocal(sp[6][:, :], sp[5][:, :]))
                        nc.vector.tensor_scalar(sp[7][:, :], sp[3][:, :], 1.0, None, ALU.is_equal)
                        wait(vec, sp_ln, b, 1, 1)
                        link(nc.vector.tensor_tensor(out=sp[8][:, :], in0=sp[4][:, :], in1=sp[6][:, :], op=ALU.mult))
                        link(nc.vector.tensor_tensor(out=sp[5][:, :], in0=sp[8][:, :], in1=sp[7][:, :], op=ALU.add))
                        link(nc.vector.tensor_tensor(out=sp[6][:, :], in0=sp[5][:, :], in1=sp[2][:, :], op=ALU.mult))
                        link(nc.vector.scalar_tensor_tensor(out=dt[:, :], in0=sp[0][:, :], scalar=0.0, in1=sp[6][:, :],
                                                            op0=ALU.max, op1=ALU.add))
                        link(nc.vector.tensor_tensor(out=da[:, :], in0=dt[:, :], in1=nega[:, :], op=ALU.mult))
                        link(nc.vector.tensor_copy(da_hi[:, :], da[:, :]))
                        nc.vector.tensor_tensor(out=da_lo[:, :], in0=da[:, :], in1=da_hi[:, :].bitcast(F32),
                                                op=ALU.subtract).then_inc(da_ready, 1)
                    if 3 <= u < 6:
                        conv_taps(u - 2)
                    if u == 8:
                        wait(vec, g_psum, b, 1, 1)
                        nc.vector.tensor_tensor(out=gm[:, :, :], in0=m1[:, :].rearrange("p (c t) -> p c t", c=C),
                                                in1=upto[:, :].unsqueeze(1).to_broadcast([P, C, P]),
                                                op=ALU.mult).then_inc(gm_ready, 1)
                        wait(vec, gm_ready, b, 1, 1)
                    if 8 <= u < 8 + C:
                        c = u - 8
                        wait(vec, decayed, b, C, c + 1)
                        nc.vector.tensor_tensor(out=mix[:, c, :, :], in0=decay[:, c, :, :],
                                                in1=gm[:, c, :].unsqueeze(1).to_broadcast([P, NH, P]),
                                                op=ALU.mult).then_inc(mixed, 1)
                    if 9 <= u < 8 + C:
                        c = u - 9
                        if c == 0:
                            wait(vec, snew_psum, b, C - 1, c + 1)
                            nc.vector.tensor_copy(state[:, 0, :], m1[:, 0:DI]).then_inc(state_ready, 1)
                        else:
                            wait(vec, state_ready, b, C - 1, c)
                            link(nc.vector.tensor_tensor(out=faded[:, c, :].rearrange("p (h d) -> p h d", h=NH),
                                                         in0=state[:, c - 1, :].rearrange("p (h d) -> p h d", h=NH),
                                                         in1=wide(edge[:, c, 1, :], HD), op=ALU.mult))
                            wait(vec, snew_psum, b, C - 1, c + 1)
                            nc.vector.tensor_tensor(out=state[:, c, :], in0=m1[:, 0:DI], in1=faded[:, c, :],
                                                    op=ALU.add).then_inc(state_ready, 1)
                    if 9 <= u < 9 + C:
                        y_chunk(u - 9)
                    if u == 13:
                        wait(vec, sq_ready, b, C, C)
                        nc.vector.tensor_scalar(ms[:, :], ss[:, :], 1.0 / DI, EPS, ALU.mult, ALU.add).then_inc(ms_ready, 1)
                    if u == 14:
                        wait(vec, rstdy_ready, b, 1, 1)
                        wait(vec, out_psum, b, 1, 1)
                        wait(vec, xo_ready, b, 1, -1)
                        for c in range(C):
                            last = nc.vector.scalar_tensor_tensor(out=x1[:, par, c, :], in0=m1[:, c * D:(c + 1) * D],
                                                                  scalar=rstdy[:, c:c + 1], in1=x[:, par, c, :],
                                                                  op0=ALU.mult, op1=ALU.add)
                        last.then_inc(x1_ready, 1)
                        wait(vec, x1_ready, b, 1, 1)
                        norm(x1[:, par, :, :], var2, rstd2, xn2)
                        norm_end(x1[:, par, :, :], rstd2, xn2)
                if q is not None:
                    accumulate(E - 1)
                if b is not None:
                    wait(vec, route_psum, b, 1, 1)
                    link(nc.vector.tensor_copy(logit[:, :, :].rearrange("p c e -> p (c e)"), m1[:, 0:C * E]))
                    nc.vector.tensor_copy(touch[:, 1:2], logit[:, 0, 0:1])
                    for c in range(C):
                        last = nc.vector.max(top[:, c, :], logit[:, c, :])
                    link(last)
                    nc.vector.tensor_tensor(out=gap[:, :], in0=top[:, :, 0], in1=top[:, :, 1], op=ALU.subtract).then_inc(gap_ready, 1)
                    for c in range(C):
                        last = nc.vector.max_index(topi[:, c, :], top[:, c, :], logit[:, c, :])
                    link(last)
                    link(nc.vector.tensor_copy(topf[:, :, :], topi[:, :, 0:2]))
                    wait(vec, tanh_ready, b, 1, 1)
                    nc.vector.tensor_scalar(wtop[:, :, 0], tanh[:, :], 0.5, 0.5, ALU.mult, ALU.add)
                    link(nc.vector.tensor_scalar(wtop[:, :, 1], tanh[:, :], -0.5, 0.5, ALU.mult, ALU.add))
                    for c in range(C):
                        last = nc.vector.tensor_scalar(pick[:, c, :], experts[:, :], topf[:, c, 0:1], wtop[:, c, 0:1],
                                                       ALU.is_equal, ALU.mult)
                    for c in range(C):
                        last = nc.vector.tensor_scalar(comb[:, par, c, :], experts[:, :], topf[:, c, 1:2], wtop[:, c, 1:2],
                                                       ALU.is_equal, ALU.mult)
                    link(last)
                    nc.vector.tensor_tensor(out=comb[:, par, :, :], in0=comb[:, par, :, :], in1=pick[:, :, :],
                                            op=ALU.add).then_inc(comb_ready, 1)
                    assert count[0] == STEPS, count[0]
                    if isinstance(b, int) and b == 0:
                        vec.wait_ge(w12_in, 16)
                        nc.vector.tensor_copy(w12_hi[:, :], w12[:, :]).then_inc(w12_ready, 1)
                        vec.wait_ge(w12_ready, 1)
                        nc.vector.tensor_tensor(out=w12_lo[:, :], in0=w12[:, :], in1=w12_hi[:, :].bitcast(F32),
                                                op=ALU.subtract).then_inc(w12_ready, 1)

            run(vec, steps)

        @block.tensor
        def _(pe):
            def split_mm(out, w, m, start=True, stop=True):
                nc.tensor.matmul(out, w[1], m[0], start=start, stop=False)
                nc.tensor.matmul(out, w[0], m[1], start=False, stop=False)
                return nc.tensor.matmul(out, w[0], m[0], start=False, stop=stop)

            pe.wait_ge(s_cs, 1)
            for r in range(6):
                last = nc.tensor.matmul(m0[:, r * B:(r + 1) * B], wmod[:, r, :], cs[:, :], start=True, stop=True)
            last.then_inc(s_mod, 1)
            pe.wait_ge(s_modt, 1)
            pe.wait_ge(const_ready, 1)

            def steps(b, par, q):
                def project_in(i):
                    if i == 1:
                        wait(pe, dt_taken, b, 1, 1)
                    if i >= 2:
                        wait(pe, tapped, b, NCT, i - 1)
                    o = DI + i * P
                    split_mm((m0, m1)[i % 2][:, :], (win_hi[:, o:o + P], win_lo[:, o:o + P]),
                             (h_hi[:, :], h_lo[:, :])).then_inc(in_psum, 1)

                def project_z(k):
                    if k == 0:
                        wait(pe, gate_taken, b, 1, 1)
                    else:
                        wait(pe, z_ready, b, 2, 1)
                    for n in range(2):
                        t = slice((2 * k + n) * P, (2 * k + n + 1) * P)
                        last = split_mm(m2[:, n * DI:(n + 1) * DI], (h_hi[:, t], h_lo[:, t]), (win_hi[:, 0:DI], win_lo[:, 0:DI]))
                    last.then_inc(z_psum, 1)

                def segments(c):
                    wait(pe, mda_ready, b, C, c + 1)
                    if c == 0:
                        wait(pe, z_ready, b, 2, 2)
                    elif c == 1:
                        wait(pe, tapped, b, NCT, 3)
                    else:
                        wait(pe, decayed, b, C, c - 1)
                    o = (m2, m0)[c % 2][:, :]
                    nc.tensor.matmul(o, after_r[:, :], mda_lo[:, c % 2, :, :].rearrange("p h t -> p (h t)"), start=True, stop=False)
                    nc.tensor.matmul(o, after_r[:, :], mda_hi[:, c % 2, :, :].rearrange("p h t -> p (h t)"), start=False,
                                     stop=True).then_inc(seg_psum, 1)

                def to_tokens(c):
                    if c == 0:
                        wait(pe, silued, b, NCT, NCT)
                        wait(pe, decayed, b, C, C)
                    else:
                        wait(pe, tok_ready, b, C, c)
                    for i in range(3):
                        last = nc.tensor.transpose(m0[:, i * P:(i + 1) * P], xbc[:, i, c * P:(c + 1) * P], ident[:, :])
                    last.then_inc(tok_psum, 1)

                def new_state(c):
                    wait(pe, xdecay_ready, b, C - 1, c + 1)
                    if c == 0:
                        wait(pe, gm_ready, b, 1, 1)
                    else:
                        wait(pe, state_ready, b, C - 1, c)
                    nc.tensor.matmul(m1[:, 0:DI], tok[:, c, DI:DI + P], xdecay[:, c, :], start=True, stop=True).then_inc(snew_psum, 1)

                def outputs(c):
                    wait(pe, mixed, b, C, c + 1)
                    wait(pe, xdt_ready, b, C, c + 1)
                    if c > 0:
                        wait(pe, y_taken, b, C, c)
                    for n in range(NH):
                        last = nc.tensor.matmul(m2[:, n * HD:(n + 1) * HD], mix[:, c, n, :], xdt[:, c, n * HD:(n + 1) * HD],
                                                start=True, stop=True)
                    if c > 0:
                        wait(pe, state_ready, b, C - 1, c)
                        last = nc.tensor.matmul(m2[:, DI:2 * DI], xbc[:, 3, c * P:(c + 1) * P], state[:, c - 1, :],
                                                start=True, stop=True)
                    last.then_inc(y_psum, 1)

                def turn_y(c):
                    wait(pe, y_ready, b, C, c + 1)
                    wait(pe, tok_ready, b, C, C)
                    if c > 0:
                        wait(pe, yt_ready, b, C, c)
                    for k in range(2):
                        last = nc.tensor.transpose(m0[:, k * P:(k + 1) * P], y[:, c, k * P:(k + 1) * P], ident[:, :])
                    last.then_inc(yt_psum, 1)

                def up(u):
                    if u == 0:
                        wait(pe, h2hi_ready, q, 1, 1)
                        wait(pe, h2lo_ready, q, 1, 1)
                    if u >= 2:
                        wait(pe, hid_ready, q, U, u - 1)
                    p2 = 1 - par
                    for k, o, s in ((0, pg, eg_psum), (1, pv, ev_psum)):
                        w = slice((2 * u + k) * P, (2 * u + k + 1) * P)
                        split_mm(o[u % 2][:, :], (w12_hi[:, w], w12_lo[:, w]), (h2_hi[:, p2, :], h2_lo[:, p2, :])).then_inc(s, 1)

                def down(e):
                    wait(pe, hid_ready, q, U, FT * (e + 1))
                    wait(pe, acc_ready, q, E, e)
                    for c in range(C):
                        for f in range(FT):
                            last = nc.tensor.matmul(po[:, c * D:(c + 1) * D], hid[:, e % 2, f, c * P:(c + 1) * P],
                                                    w3[:, FT * e + f, :], start=(f == 0), stop=(f == FT - 1))
                    last.then_inc(o_psum, 1)

                for u in range(U):
                    if q is not None:
                        up(u)
                        if u >= 2 and u % 2 == 0:
                            down(u // 2 - 1)
                    if b is None:
                        continue
                    if u == 0:
                        wait(pe, acc_started, b, 1)
                        wait(pe, comb_ready, b, 1)
                        wait(pe, h2lo_ready, b, 1)
                        wait(pe, gcol, b, 1, 1)
                        for k, r in ((0, GA), (1, GB)):
                            last = nc.tensor.matmul(m2[:, k * D:(k + 1) * D], ccol[:, :], wmod[:, r, :], start=True, stop=True)
                        last.then_inc(gate_psum, 1)
                    if u == 1:
                        wait(pe, xn1, b, 1, 1)
                        for c in range(C):
                            last = nc.tensor.transpose(m0[:, c * P:(c + 1) * P], xn[:, c, :], ident[:, :])
                        last.then_inc(ht_psum, 1)
                    if u == 2:
                        wait(pe, hhi_ready, b, 1, 1)
                        wait(pe, hlo_ready, b, 1, 1)
                        for c in range(C):
                            t = slice(c * P, (c + 1) * P)
                            last = split_mm(m1[:, c * NH:(c + 1) * NH], (h_hi[:, t], h_lo[:, t]), (win_hi[:, 768:772], win_lo[:, 768:772]))
                        last.then_inc(dt_psum, 1)
                        project_in(0)
                    if u == 3:
                        project_in(1)
                        project_z(0)
                    if u == 4:
                        project_in(2)
                        project_z(1)
                    if u == 5:
                        project_in(3)
                    if u == 6:
                        wait(pe, tapped, b, NCT, NCT)
                        wait(pe, da_ready, b, 1, 1)
                        for c in range(C):
                            for k, w in enumerate((upto_r, ones_r)):
                                o = m1[:, (2 * c + k) * NH:(2 * c + k + 1) * NH]
                                nc.tensor.matmul(o, w[:, :], da_lo[:, c * NH:(c + 1) * NH], start=True, stop=False)
                                last = nc.tensor.matmul(o, w[:, :], da_hi[:, c * NH:(c + 1) * NH], start=False, stop=True)
                        last.then_inc(edge_psum, 1)
                        segments(0)
                        segments(1)
                    if u == 7:
                        segments(2)
                        segments(3)
                    if u == 8:
                        wait(pe, edge_ready, b, 1, 1)
                        wait(pe, silued, b, NCT, NCT)
                        for c in range(C):
                            t = slice(c * P, (c + 1) * P)
                            last = nc.tensor.matmul(m1[:, t], xbc[:, 2, t], xbc[:, 3, t], start=True, stop=True)
                        last.then_inc(g_psum, 1)
                    for c in {8: (0, 1), 9: (2, 3)}.get(u, ()):
                        to_tokens(c)
                    if 9 <= u < 8 + C:
                        new_state(u - 9)
                    if 9 <= u < 9 + C:
                        outputs(u - 9)
                    if 10 <= u < 10 + C:
                        turn_y(u - 10)
                    if u == 13:
                        wait(pe, wo_ready, b, 1, 1)
                        wait(pe, state_ready, b, C - 1, C - 1)
                        wait(pe, yt_ready, b, C, C)
                        for c in range(C):
                            for k in range(2):
                                last = nc.tensor.matmul(m1[:, c * D:(c + 1) * D], yt[:, c, k, :], wo[:, k, :], start=(k == 0),
                                                        stop=(k == 1))
                        last.then_inc(out_psum, 1)
                if b is not None:
                    wait(pe, xn2, b, 1, 1)
                    for c in range(C):
                        last = nc.tensor.transpose(m0[:, c * P:(c + 1) * P], xn[:, c, :], ident[:, :])
                    last.then_inc(h2t_psum, 1)
                if q is not None:
                    down(E - 1)
                if b is not None:
                    wait(pe, h2_ready, b, 1, 1)
                    for c in range(C):
                        last = nc.tensor.matmul(m1[:, c * E:(c + 1) * E], h2[:, c * P:(c + 1) * P], wg[:, :], start=True, stop=True)
                    last.then_inc(route_psum, 1)
                    wait(pe, comb_ready, b, 1, 1)
                    for c in range(C):
                        last = nc.tensor.transpose(m1[0:E, c * P:(c + 1) * P], comb[:, par, c, :], ident[:, :])
                    last.then_inc(combt_psum, 1)
                    wait(pe, combt_ready, b, 1, 1)
                    wait(pe, y_taken, b, C, C)
                    for c in range(C):
                        last = nc.tensor.matmul(m2[:, c * D:(c + 1) * D], combt[:, c * P:(c + 1) * P], b3[:, :], start=True, stop=True)
                    last.then_inc(b3_psum, 1)

                if isinstance(b, int) and b == 0:
                    pe.wait_ge(w12_ready, 2)
                    pe.wait_ge(w3_in, 16)

            run(pe, steps)


def kernel(**inputs):
    import numpy as np
    import concourse.bacc as bacc
    from concourse.bass_utils import run_bass_kernel_spmd as launch

    g = {k.replace("L0_attn_", "").replace("L0_ffn_", "f_").replace("L0_", ""): np.asarray(v) for k, v in inputs.items()}
    arr = np.ascontiguousarray
    to = lambda v, n: np.broadcast_to(v, (n,) + v.shape)
    cols = np.concatenate([
        g["conv_w"].reshape(NCT, P, KC).transpose(1, 0, 2).reshape(P, NCT * KC),
        g["conv_b"].reshape(NCT, P).T,
        np.stack([g["f_b1"].reshape(U, P), g["f_b2"].reshape(U, P)], 1).reshape(2 * U, P).T,
        g["norm_w"].reshape(2, P).T], axis=1)
    rows = np.concatenate([np.tile(g["dt_bias"], C), np.tile(g["A_log"], C), np.tile(g["A_log"], C), np.repeat(g["D"], HD)])
    data = {
        "x": g["X"],
        "win": arr(g["W_in"].T),
        "wout": arr(g["W_out"].T.reshape(2, P, D).transpose(1, 0, 2)),
        "w12": arr(np.stack([g["f_W1"].reshape(U, P, D), g["f_W2"].reshape(U, P, D)], 1).reshape(2 * U * P, D).T),
        "w3": arr(g["f_W3"].transpose(0, 2, 1).reshape(U, P, D).transpose(1, 0, 2)),
        "wg": arr(g["f_Wg"].T),
        "b3": g["f_b3"],
        "wmod": arr(g["wmod"].reshape(D, 6, D)),
        "ct": arr(g["c"].T),
        "cols": arr(cols),
        "rows": arr(to(rows, P)),
        "ident": np.eye(P, dtype=np.float32),
        "upto": np.triu(np.ones((P, P), np.float32)),
        "after": np.tril(np.ones((P, P), np.float32), -1),
        "expo": np.full((P, C), -0.5, np.float32),
        "experts": arr(to(np.arange(E, dtype=np.float32), P)),
    }
    nc = bacc.Bacc("TRN2", target_bir_lowering=False, num_devices=1)
    aps = {k: nc.dram_tensor(f"in_{k}", v.shape, mybir.dt.from_np(v.dtype), kind="ExternalInput").ap() for k, v in data.items()}
    aps["out"] = nc.dram_tensor("out", (B, L, D), F32, kind="ExternalOutput").ap()
    program(nc, aps)
    r = launch(nc, [{f"in_{k}": v for k, v in data.items()}], core_ids=[0])
    return r.results[0]["out"]
```

```python
import math
from contextlib import ExitStack

import concourse.bass as bass
from concourse import mybir

ALU = mybir.AluOpType
ACT = mybir.ActivationFunctionType
F32 = mybir.dt.float32
F32R = mybir.dt.float32r
U32 = mybir.dt.uint32

P = 128
B = 16
L = 512
C = L // P
D = 128
DI = 256
NH = 4
HD = DI // NH
NCT = 4
NIN = 2 * DI + 2 * P + NH
KC = 4
E = 8
FT = 2
U = E * FT
EPS = 1e-5
SA, CA, GA, SB, CB, GB = range(6)

TABLE = (("ident", P), ("upto", P), ("after", P), ("expo", C), ("experts", E), ("conv_w", NCT * KC), ("conv_b", NCT),
         ("b12", 2 * U), ("norm_w", 2), ("dt_bias", C * NH), ("a_log", C * NH), ("d_row", DI), ("ct", B), ("wg", E))
NTABLE = sum(n for _, n in TABLE)


def program(nc, d):
    ctx = ExitStack()
    with ctx:
        def sb(name, shape, dt=F32):
            return ctx.enter_context(nc.sbuf_tensor(name, shape, dt))

        def bank(name):
            return ctx.enter_context(nc.psum_tensor(name, [P, 512], F32))

        def sem(name):
            return ctx.enter_context(nc.semaphore(name))

        table = sb("table", [P, NTABLE])
        upto_r = sb("upto_r", [P, P], F32R)
        after_r = sb("after_r", [P, P], F32R)
        ones_r = sb("ones_r", [P, P], F32R)
        win = sb("win", [P, NIN])
        win_hi = sb("win_hi", [P, NIN], F32R)
        win_lo = sb("win_lo", [P, NIN], F32R)
        w12 = sb("w12", [P, 2 * U * P])
        w12_hi = sb("w12_hi", [P, 2 * U * P], F32R)
        w12_lo = sb("w12_lo", [P, 2 * U * P], F32R)
        w3 = sb("w3", [P, U, D])
        wout = sb("wout", [P, 2, D])
        woutn = sb("woutn", [P, 2, D])
        b3 = sb("b3", [E, D])
        wmod = sb("wmod", [P, 6, D])
        cs = sb("cs", [P, B])
        mod = sb("mod", [P, 6, B])
        nega = sb("nega", [P, C * NH])
        euler = sb("euler", [P, C * NH])

        part, start = {}, 0
        for name, n in TABLE:
            part[name] = table[:, start:start + n]
            start += n
        ident = part["ident"]
        upto, after = part["upto"], part["after"]
        expo, experts = part["expo"], part["experts"]
        conv_w, conv_b, b12, norm_w = part["conv_w"], part["conv_b"], part["b12"], part["norm_w"]
        dt_bias, a_log, d_row = part["dt_bias"], part["a_log"], part["d_row"]
        ct, wg = part["ct"], part["wg"]

        x = sb("x", [P, 2, C, D])
        touch = sb("touch", [P, 2])
        stats = sb("stats", [P, C, 6])
        mv = sb("mv", [P, C, 2])
        var = sb("var", [P, C])
        rstd = sb("rstd", [P, C])
        xn = sb("xn", [P, C, D])
        next_mv = sb("next_mv", [P, C, 2])
        next_var = sb("next_var", [P, C])
        next_rstd = sb("next_rstd", [P, C])
        next_xn = sb("next_xn", [P, C, D])
        h = sb("h", [P, L])
        h_hi = sb("h_hi", [P, L], F32R)
        h_lo = sb("h_lo", [P, L], F32R)
        gate_raw = sb("gate_raw", [B, 2 * D])
        gate_sign = sb("gate_sign", [B, 2 * D])
        gate_size = sb("gate_size", [B, 2 * D])
        gate_all = sb("gate_all", [B, 2 * D])
        gate = sb("gate", [P, 2, 2 * D])
        wo = sb("wo", [P, 2, D])
        raw = sb("raw", [P, C * NH])
        raw_pos = sb("raw_pos", [P, C * NH])
        neg_abs = sb("neg_abs", [P, C * NH])
        exp_neg = sb("exp_neg", [P, C * NH])
        two_plus = sb("two_plus", [P, C * NH])
        inverse = sb("inverse", [P, C * NH])
        arg = sb("arg", [P, C * NH])
        arg_sq = sb("arg_sq", [P, C * NH])
        series = sb("series", [P, C * NH])
        exp_a = sb("exp_a", [P, C * NH])
        dt = sb("dt", [P, C * NH])
        da = sb("da", [P, C * NH])
        da_hi = sb("da_hi", [P, C * NH], F32R)
        da_lo = sb("da_lo", [P, C * NH], F32R)
        mda_hi = sb("mda_hi", [P, 2, NH, P], F32R)
        mda_lo = sb("mda_lo", [P, 2, NH, P], F32R)
        decay = sb("decay", [P, C, NH, P])
        edge = sb("edge", [P, 2, C, NH])
        xbc = sb("xbc", [P, NCT, L])
        zs = sb("zs", [P, C, DI])
        tok = sb("tok", [P, C, DI + P])
        xdt = sb("xdt", [P, C, DI])
        xdecay = sb("xdecay", [P, C, DI])
        xskip = sb("xskip", [P, C, DI])
        gm = sb("gm", [P, C, P])
        mix = sb("mix", [P, C, NH, P])
        state = sb("state", [P, C - 1, DI])
        faded = sb("faded", [P, C - 1, DI])
        ysum = sb("ysum", [P, C, DI])
        y = sb("y", [P, C, DI])
        ss = sb("ss", [P, C])
        ms = sb("ms", [P, C])
        rstdy = sb("rstdy", [P, C])
        yt = sb("yt", [P, C, 2, P])
        x1 = sb("x1", [P, 2, C, D])
        h2 = sb("h2", [P, L])
        h2_hi = sb("h2_hi", [P, 2, L], F32R)
        h2_lo = sb("h2_lo", [P, 2, L], F32R)
        logit = sb("logit", [P, C, E])
        top = sb("top", [P, C, E])
        topi = sb("topi", [P, C, E], U32)
        topf = sb("topf", [P, C, 2])
        gap = sb("gap", [P, C])
        tanh = sb("tanh", [P, C])
        wtop = sb("wtop", [P, C, 2])
        pick = sb("pick", [P, C, E])
        comb = sb("comb", [P, 2, C, E])
        combt = sb("combt", [E, L])
        sg = sb("sg", [P, 2, L])
        acc = sb("acc", [P, 2, C, D])
        hid = w12[:, 0:2 * FT * L].rearrange("p (k f t) -> p k f t", k=2, f=FT)
        eo = w12[:, 2 * FT * L:2 * FT * L + 2 * C * D].rearrange("p (k c m) -> p k c m", k=2, c=C)
        xo = w12[:, 2 * FT * L + 2 * C * D:].rearrange("p (k c m) -> p k c m", k=2, c=C)

        m0, m1, m2 = bank("m0"), bank("m1"), bank("m2")
        pg = [bank("pg0"), bank("pg1")]
        pv = [bank("pv0"), bank("pv1")]
        po = bank("po")
        in_bank, seg_bank, tok_bank = (m0, m1, m0, m2), (m1, m0, m2, m1), (m0, m1)

        consts_in, win_in, w12_in, w3_in = sem("consts_in"), sem("win_in"), sem("w12_in"), sem("w3_in")
        s_vec, s_act = sem("setup_vector_step"), sem("setup_scalar_step")
        s_cs, s_mod, s_modt = sem("silu_c_ready"), sem("mod_psum"), sem("mod_ready")
        w12_hi_ready, w12_lo_ready = sem("w12_hi_ready"), sem("w12_lo_ready")
        const_ready = sem("constants_ready")
        x_in, x_out = sem("x_loaded"), sem("x_stored")
        acc_started, eo_ready = sem("acc_started"), sem("eo_ready")
        vec_step = sem("vector_step")
        gate_psum, gate_step, gates_out = sem("gate_psum"), sem("gate_step"), sem("gates_stored")
        gate_in, wo_ready = sem("gate_loaded"), sem("wo_ready")
        norm1_var, norm1_rstd, norm1_ready, ht_psum = sem("norm1_var"), sem("norm1_rstd"), sem("norm1_ready"), sem("ht_psum")
        h_ready, hhi_ready, hlo_ready = sem("h_ready"), sem("hhi_ready"), sem("hlo_ready")
        dt_psum, dt_taken = sem("dt_psum"), sem("dt_taken")
        neg_abs_ready, exp_neg_ready, da_ready = sem("neg_abs_ready"), sem("exp_neg_ready"), sem("da_ready")
        in_psum, tap0, tapped, silued = sem("in_psum"), sem("tap0"), sem("tapped"), sem("silued")
        z_psum, z_ready = sem("z_psum"), sem("z_ready")
        mda_ready, seg_psum, decayed = sem("mda_ready"), sem("seg_psum"), sem("decayed")
        edge_psum, edge_ready = sem("edge_psum"), sem("edge_ready")
        g_psum, gm_ready, mixed = sem("g_psum"), sem("gm_ready"), sem("mixed")
        tok_psum = sem("tok_psum")
        tok_ready, late_tok_ready = sem("tok_ready"), sem("late_tok_ready")
        xdt_ready, xdecay_ready, xskip_ready = sem("xdt_ready"), sem("xdecay_ready"), sem("xskip_ready")
        snew_psum, state_ready = sem("snew_psum"), sem("state_ready")
        y_psum, y_taken, y_ready, sq_ready = sem("y_psum"), sem("y_taken"), sem("y_ready"), sem("sq_ready")
        yt_psum, yt_ready, out_psum = sem("yt_psum"), sem("yt_ready"), sem("out_psum")
        ms_ready, rstdy_ready, x1_ready = sem("ms_ready"), sem("rstdy_ready"), sem("x1_ready")
        norm2_var, norm2_rstd, norm2_ready, h2t_psum = sem("norm2_var"), sem("norm2_rstd"), sem("norm2_ready"), sem("h2t_psum")
        h2_ready, h2hi_ready, h2lo_ready = sem("h2_ready"), sem("h2hi_ready"), sem("h2lo_ready")
        route_psum, gap_ready, tanh_ready = sem("route_psum"), sem("gap_ready"), sem("tanh_ready")
        comb_ready, combt_psum, combt_ready, b3_psum = sem("comb_ready"), sem("combt_psum"), sem("combt_ready"), sem("b3_psum")
        eg_psum, ev_psum, sg_ready, hid_ready = sem("eg_psum"), sem("ev_psum"), sem("sg_ready"), sem("hid_ready")
        o_psum, acc_ready = sem("o_psum"), sem("acc_ready")
        gated_ready, xo_ready = sem("gated_ready"), sem("xo_ready")

        def wait(eng, s, b, per, n=0):
            v = b * per + n
            if not isinstance(v, int) or v > 0:
                eng.wait_ge(s, v)

        def unit_w(u):
            return slice(2 * u * P, 2 * (u + 1) * P)

        def wide(ap, n):
            return ap.unsqueeze(2).to_broadcast([P, ap.shape[1], n])

        def run(eng, steps):
            steps(0, 0, None)
            steps(1, 1, 0)
            with eng.Fori(0, (B - 4) // 2) as j:
                for k in range(2):
                    steps(2 * j + 2 + k, k, 2 * j + 1 + k)
            steps(B - 2, 0, B - 3)
            steps(B - 1, 1, B - 2)
            steps(None, 0, B - 1)

        block = ctx.enter_context(nc.Block())

        @block.sync
        def _(sp_):
            xv = d["x"].rearrange("b (c p) m -> b p c m", p=P)
            ov = d["out"].rearrange("b (c p) m -> b p c m", p=P)
            sp_.dma_start(x[:, 0, :, :], xv[0]).then_inc(x_in, 16)
            for dst, src in ((table[:, :], "table"), (wmod[:, :, :], "wmod"), (wout[:, :, :], "wout"),
                             (b3[:, :], "b3")):
                sp_.dma_start(dst, d[src]).then_inc(consts_in, 16)

            def load(n, par):
                if not isinstance(n, int) or n >= 2:
                    sp_.wait_ge(x1_ready, n - 1)
                else:
                    sp_.wait_ge(norm1_var, 1)
                sp_.dma_start(x[:, par, :, :], xv[n]).then_inc(x_in, 16)

            def store(n, par):
                sp_.wait_ge(xo_ready, n + 1)
                sp_.dma_start(ov[n], xo[:, par, :, :]).then_inc(x_out, 16)

            def load_gate(n, par):
                if not isinstance(n, int) or n >= 2:
                    sp_.wait_ge(xo_ready, n - 1)
                sp_.dma_start(gate[:, par, :], d["gates"][n].partition_broadcast(P)).then_inc(gate_in, 16)

            sp_.wait_ge(gate_step, 4)
            sp_.dma_start(d["gates"], gate_all[:, :]).then_inc(gates_out, 16)
            sp_.wait_ge(gates_out, 16)
            load_gate(0, 0)
            load(1, 1)
            sp_.wait_ge(gate_in, 16)
            load_gate(1, 1)
            load(2, 0)
            load(3, 1)
            store(0, 0)
            load_gate(2, 0)
            load(4, 0)
            store(1, 1)
            load_gate(3, 1)
            with sp_.Fori(0, (B - 6) // 2) as j:
                for k in range(2):
                    load(2 * j + 5 + k, 1 - k)
                    store(2 * j + 2 + k, k)
                    load_gate(2 * j + 4 + k, k)
            load(B - 1, 1)
            for n in range(B - 4, B):
                store(n, n % 2)
                if n + 2 < B:
                    load_gate(n + 2, n % 2)
            sp_.wait_ge(x_out, 16 * B)

        @block.gpsimd
        def _(pool):
            pool.dma_start(win[:, :], d["win"]).then_inc(win_in, 16)
            pool.wait_ge(win_in, 16)
            pool.wait_ge(consts_in, 16 * 4)
            pool.dma_start(w12[:, :], d["w12"]).then_inc(w12_in, 16)
            pool.dma_start(w3[:, :, :], d["w3"]).then_inc(w3_in, 16)
            pool.wait_ge(const_ready, 1)

            def power(dst, src, ready, b, done):
                wait(pool, ready, b, 1, 1)
                nc.gpsimd.tensor_tensor(out=dst[:, :], in0=src[:, :], in1=expo[:, :], op=ALU.pow).then_inc(done, 1)

            def steps(b, par, q):
                def add_expert(e):
                    p2 = 1 - par
                    wait(pool, eo_ready, q, E, e + 1)
                    if e > 0:
                        wait(pool, acc_ready, q, E, e)
                    nc.gpsimd.tensor_tensor(out=acc[:, p2, :, :], in0=acc[:, p2, :, :], in1=eo[:, e % 2, :, :],
                                            op=ALU.add).then_inc(acc_ready, 1)

                if isinstance(b, int) and b == 0:
                    power(next_rstd, next_var, norm1_var, 0, norm1_rstd)
                for u in range(U):
                    if q is not None and u in (4, 6, 14):
                        add_expert(u // 2 - 2)
                    if b is not None:
                        if u == 1:
                            wait(pool, neg_abs_ready, b, 1, 1)
                            nc.gpsimd.tensor_tensor(out=exp_neg[:, :], in0=euler[:, :], in1=neg_abs[:, :], op=ALU.pow).then_inc(exp_neg_ready, 1)
                        for c in {3: (0, 1), 5: (2, 3)}.get(u, ()):
                            if c == 0:
                                wait(pool, da_ready, b, 1, 1)
                            if c >= 2:
                                wait(pool, seg_psum, b, C, c - 1)
                            for dst, src in ((mda_hi, da_hi), (mda_lo, da_lo)):
                                last = nc.gpsimd.tensor_tensor(out=dst[:, c % 2, :, :],
                                                               in0=upto[:, :].unsqueeze(1).to_broadcast([P, NH, P]),
                                                               in1=wide(src[:, c * NH:(c + 1) * NH].bitcast(F32), P), op=ALU.mult)
                            last.then_inc(mda_ready, 1)
                        if 7 <= u < 7 + C:
                            c = u - 7
                            if c < 2:
                                wait(pool, tok_ready, b, 2, c + 1)
                            else:
                                wait(pool, late_tok_ready, b, 2, c - 1)
                            wait(pool, decayed, b, C, c + 1)
                            xt = tok[:, c, 0:DI].rearrange("p (h d) -> p h d", h=NH)
                            nc.gpsimd.tensor_tensor(out=xdt[:, c, :].rearrange("p (h d) -> p h d", h=NH), in0=xt,
                                                    in1=wide(dt[:, c * NH:(c + 1) * NH], HD), op=ALU.mult).then_inc(xdt_ready, 1)
                            if c < C - 1:
                                wait(pool, xdt_ready, b, C, c + 1)
                                nc.gpsimd.tensor_tensor(out=xdecay[:, c, :].rearrange("p (h d) -> p h d", h=NH),
                                                        in0=xdt[:, c, :].rearrange("p (h d) -> p h d", h=NH),
                                                        in1=wide(decay[:, c, :, P - 1], HD), op=ALU.mult).then_inc(xdecay_ready, 1)
                            nc.gpsimd.tensor_tensor(out=xskip[:, c, :], in0=tok[:, c, 0:DI], in1=d_row,
                                                    op=ALU.mult).then_inc(xskip_ready, 1)
                        if u == 12:
                            power(rstdy, ms, ms_ready, b, rstdy_ready)
                        if u == 12 and not (isinstance(b, int) and b == B - 1):
                            power(next_rstd, next_var, norm1_var, b + 1, norm1_rstd)
                        if u == 13:
                            power(rstd, var, norm2_var, b, norm2_rstd)
                        if u == 15:
                            wait(pool, h2hi_ready, b, 1, 1)
                            nc.gpsimd.tensor_tensor(out=h2_lo[:, par, :], in0=h2[:, :], in1=h2_hi[:, par, :].bitcast(F32),
                                                    op=ALU.subtract).then_inc(h2lo_ready, 1)
                    if q is not None and u in (8, 10, 12):
                        add_expert(u // 2 - 2)
                    if isinstance(b, int) and b == 0:
                        pool.wait_ge(w12_hi_ready, u + 1)
                        nc.gpsimd.tensor_tensor(out=w12_lo[:, unit_w(u)], in0=w12[:, unit_w(u)],
                                                in1=w12_hi[:, unit_w(u)].bitcast(F32), op=ALU.subtract).then_inc(w12_lo_ready, 1)
                if isinstance(b, int) and b == 0:
                    pool.wait_ge(w12_lo_ready, U)
                if q is not None:
                    add_expert(E - 2)
                    add_expert(E - 1)
                    p2 = 1 - par
                    wait(pool, acc_ready, q, E, E)
                    wait(pool, x_out, q, 16)
                    nc.gpsimd.tensor_tensor(out=xo[:, p2, :, :], in0=acc[:, p2, :, :],
                                            in1=gate[:, p2, D:2 * D].unsqueeze(1).to_broadcast([P, C, D]),
                                            op=ALU.mult).then_inc(gated_ready, 1)
                    wait(pool, gated_ready, q, 1, 1)
                    nc.gpsimd.tensor_tensor(out=xo[:, p2, :, :], in0=xo[:, p2, :, :], in1=x1[:, p2, :, :],
                                            op=ALU.add).then_inc(xo_ready, 1)

            run(pool, steps)

        @block.scalar
        def _(act):
            act.wait_ge(consts_in, 16 * 4)
            nc.scalar.activation(exp_a[:, :], a_log, ACT.Exp).then_inc(s_act, 1)
            nc.scalar.activation(cs[:, :], ct[:, :], ACT.Silu).then_inc(s_cs, 1)
            act.wait_ge(s_mod, 1)
            for r in (SA, SB):
                nc.scalar.activation(mod[:, r, :], m0[:, r * B:(r + 1) * B], ACT.Copy)
            for r in (CA, CB):
                last = nc.scalar.activation(mod[:, r, :], m0[:, r * B:(r + 1) * B], ACT.Copy, bias=1.0)
            last.then_inc(s_modt, 1)
            act.wait_ge(s_modt, 1)
            act.wait_ge(s_act, 1)

            def steps(b, par, q):
                def expert_silu(u):
                    wait(act, eg_psum, q, U, u + 1)
                    wait(act, hid_ready, q, U, max(u - 1, 0))
                    nc.scalar.activation(sg[:, u % 2, :], pg[u % 2][:, :], ACT.Silu,
                                         bias=b12[:, 2 * u:2 * u + 1]).then_inc(sg_ready, 1)

                def conv_first(i):
                    wait(act, in_psum, b, NCT, i + 1)
                    nc.scalar.activation(xbc[:, i, :], in_bank[i][:, :], ACT.Identity, bias=conv_b[:, i:i + 1],
                                         scale=conv_w[:, i * KC + KC - 1:i * KC + KC]).then_inc(tap0, 1)

                def conv_silu(i):
                    wait(act, tapped, b, NCT, i + 1)
                    nc.scalar.activation(xbc[:, i, :], xbc[:, i, :], ACT.Silu).then_inc(silued, 1)

                def z_silu(k):
                    wait(act, z_psum, b, 2, k + 1)
                    nc.scalar.activation(zs[:, 2 * k:2 * k + 2, :].rearrange("p c e -> p (c e)"), m2[:, :],
                                         ACT.Silu).then_inc(z_ready, 1)

                def weigh(e):
                    p2 = 1 - par
                    wait(act, o_psum, q, E, e + 1)
                    wait(act, acc_ready, q, E, max(e - 1, 0))
                    for c in range(C):
                        last = nc.scalar.activation(eo[:, e % 2, c, :], po[:, c * D:(c + 1) * D], ACT.Copy,
                                                    scale=comb[:, p2, c, e:e + 1])
                    last.then_inc(eo_ready, 1)

                def first_input(n):
                    wait(act, route_psum, n, 1)
                    wait(act, ht_psum, n, 1, 1)
                    nc.scalar.activation(h[:, :], m0[:, :], ACT.Identity, bias=mod[:, SA, bass.ds(n, 1)],
                                         scale=mod[:, CA, bass.ds(n, 1)]).then_inc(h_ready, 1)

                if isinstance(b, int) and b == 0:
                    first_input(0)

                def take_tokens(c):
                    wait(act, tok_psum, b, C, c + 1)
                    nc.scalar.activation(tok[:, c, :], tok_bank[c % 2][:, 0:DI + P], ACT.Copy).then_inc(tok_ready, 1)

                for u in range(U):
                    if b is not None and u == 7:
                        take_tokens(0)
                        take_tokens(1)
                    if q is not None:
                        expert_silu(u)
                        if u == 1:
                            wait(act, combt_psum, q, 1, 1)
                            nc.scalar.activation(combt[:, :], po[0:E, :], ACT.Copy).then_inc(combt_ready, 1)
                        if u == 2:
                            wait(act, b3_psum, q, 1, 1)
                            wait(act, xo_ready, q, 1)
                            nc.scalar.activation(acc[:, 1 - par, :, :].rearrange("p c m -> p (c m)"), po[:, :],
                                                 ACT.Copy).then_inc(acc_started, 1)
                        if u >= 4 and u % 2 == 0:
                            weigh(u // 2 - 2)
                    if b is None:
                        continue
                    if u == 1:
                        conv_first(0)
                    if u == 2:
                        conv_first(1)
                        z_silu(0)
                    if u == 3:
                        conv_first(2)
                        conv_silu(0)
                        z_silu(1)
                    if u == 4:
                        conv_first(3)
                        conv_silu(1)
                    if u == 5:
                        conv_silu(2)
                    if u == 6:
                        conv_silu(3)
                        for c in range(C):
                            wait(act, seg_psum, b, C, c + 1)
                            nc.scalar.activation(decay[:, c, :, :].rearrange("p h t -> p (h t)"), seg_bank[c][:, :],
                                                 ACT.Exp).then_inc(decayed, 1)
                        wait(act, edge_psum, b, 1, 1)
                        nc.scalar.activation(edge[:, :, :, :].rearrange("p k c h -> p (k c h)"), m0[:, 0:2 * C * NH],
                                             ACT.Exp).then_inc(edge_ready, 1)
                    if 9 <= u < 9 + C:
                        c = u - 9
                        wait(act, y_ready, b, C, c + 1)
                        nc.scalar.activation(ysum[:, c, :], y[:, c, :], ACT.Square, accum_out=ss[:, c:c + 1]).then_inc(sq_ready, 1)
                        wait(act, yt_psum, b, C, c + 1)
                        nc.scalar.activation(yt[:, c, :, :].rearrange("p k t -> p (k t)"), m0[:, 0:DI],
                                             ACT.Copy).then_inc(yt_ready, 1)
                    if u == 15:
                        wait(act, h2t_psum, b, 1, 1)
                        nc.scalar.activation(h2[:, :], m0[:, :], ACT.Identity, bias=mod[:, SB, bass.ds(b, 1)],
                                             scale=mod[:, CB, bass.ds(b, 1)]).then_inc(h2_ready, 1)
                    if isinstance(b, int) and b == 0:
                        act.wait_ge(w12_in, 16)
                        nc.scalar.activation(w12_hi[:, unit_w(u)], w12[:, unit_w(u)], ACT.Copy).then_inc(w12_hi_ready, 1)
                if isinstance(b, int) and b == 0:
                    act.wait_ge(w12_lo_ready, U)
                if q is not None:
                    weigh(E - 2)
                if b is not None and not (isinstance(b, int) and b == B - 1):
                    first_input(b + 1)
                if b is not None:
                    wait(act, gap_ready, b, 1, 1)
                    nc.scalar.activation(tanh[:, :], gap[:, :], ACT.Tanh, scale=0.5).then_inc(tanh_ready, 1)
                if q is not None:
                    weigh(E - 1)

            run(act, steps)

        @block.vector
        def _(vec):
            def set_up():
                vec.wait_ge(win_in, 16)
                nc.vector.tensor_copy(win_hi[:, :], win[:, :]).then_inc(s_vec, 1)
                vec.wait_ge(s_vec, 1)
                nc.vector.tensor_tensor(out=win_lo[:, :], in0=win[:, :], in1=win_hi[:, :].bitcast(F32), op=ALU.subtract)
                vec.wait_ge(consts_in, 16 * 4)
                nc.vector.tensor_copy(upto_r[:, :], upto[:, :])
                nc.vector.tensor_copy(after_r[:, :], after[:, :])
                nc.vector.tensor_scalar(ones_r[:, :], upto[:, :], 0.0, 1.0, ALU.mult, ALU.add)
                nc.vector.tensor_scalar(euler[:, :], upto[:, 0:C * NH], 0.0, math.e, ALU.mult, ALU.add)
                for k in range(2):
                    nc.vector.tensor_scalar(woutn[:, k, :], wout[:, k, :], norm_w[:, k:k + 1], None, ALU.mult)
                vec.wait_ge(s_act, 1)
                nc.vector.tensor_scalar(nega[:, :], exp_a[:, :], -1.0, None, ALU.mult).then_inc(const_ready, 1)

            def all_gates():
                vec.wait_ge(gate_psum, 1)
                nc.vector.tensor_scalar(gate_sign[:, :], m2[0:B, 0:2 * D], 0.0, 2.0, ALU.is_ge, ALU.mult).then_inc(gate_step, 1)
                vec.wait_ge(gate_step, 1)
                nc.vector.scalar_tensor_tensor(out=gate_raw[:, :], in0=gate_sign[:, :], scalar=-1.0, in1=m2[0:B, 0:2 * D],
                                               op0=ALU.add, op1=ALU.mult).then_inc(gate_step, 1)
                vec.wait_ge(gate_step, 2)
                nc.vector.tensor_scalar(gate_size[:, :], gate_raw[:, :], 0.25, None, ALU.max).then_inc(gate_step, 1)
                vec.wait_ge(gate_step, 3)
                nc.vector.scalar_tensor_tensor(out=gate_all[:, :], in0=gate_sign[:, :], scalar=-1.0, in1=gate_size[:, :],
                                               op0=ALU.add, op1=ALU.mult).then_inc(gate_step, 1)

            LAST = 15
            STEPS = 41

            def steps(b, par, q):
                count = [0]

                def link(ins):
                    count[0] += 1
                    ins.then_inc(vec_step, 1)
                    wait(vec, vec_step, b, STEPS, count[0])

                def norm(src, mv, var, ready_var):
                    for c in range(C):
                        last = nc.vector.bn_stats(stats[:, c, :], src[:, c, :])
                    link(last)
                    nc.vector.tensor_copy(touch[:, 0:1], stats[:, 0, 0:1])
                    for c in range(C):
                        last = nc.vector.bn_aggr(mv[:, c, :], stats[:, c, :])
                    link(last)
                    nc.vector.tensor_scalar(var[:, :], mv[:, :, 1], EPS, None, ALU.add).then_inc(ready_var, 1)

                def norm_end(dst, src, mv, rstd, ready_rstd, n, done):
                    wait(vec, ready_rstd, n, 1, 1)
                    for c in range(C):
                        last = nc.vector.tensor_scalar(dst[:, c, :], src[:, c, :], mv[:, c, 0:1], rstd[:, c:c + 1],
                                                       ALU.subtract, ALU.mult)
                    last.then_inc(done, 1)

                def conv_taps(i):
                    wait(vec, tap0, b, NCT, i + 1)
                    for k in range(1, KC):
                        w = conv_w[:, i * KC + KC - 1 - k:i * KC + KC - k]
                        last = nc.vector.scalar_tensor_tensor(out=xbc[:, i, k:L], in0=in_bank[i][:, 0:L - k], scalar=w,
                                                              in1=xbc[:, i, k:L], op0=ALU.mult, op1=ALU.add)
                        if k < KC - 1:
                            link(last)
                    last.then_inc(tapped, 1)

                def mix_chunk(c):
                    wait(vec, decayed, b, C, c + 1)
                    nc.vector.tensor_tensor(out=mix[:, c, :, :], in0=decay[:, c, :, :],
                                            in1=gm[:, c, :].unsqueeze(1).to_broadcast([P, NH, P]),
                                            op=ALU.mult).then_inc(mixed, 1)

                def y_chunk(c):
                    wait(vec, y_psum, b, C, c + 1)
                    wait(vec, xskip_ready, b, C, c + 1)
                    if c == 0:
                        nc.vector.tensor_tensor(out=ysum[:, c, :], in0=m2[:, 0:DI], in1=xskip[:, c, :],
                                                op=ALU.add).then_inc(y_taken, 1)
                        wait(vec, y_taken, b, C, c + 1)
                    else:
                        link(nc.vector.tensor_tensor(out=ysum[:, c, :].rearrange("p (h d) -> p h d", h=NH),
                                                     in0=m2[:, DI:2 * DI].rearrange("p (h d) -> p h d", h=NH),
                                                     in1=wide(edge[:, 0, c, :], HD), op=ALU.mult))
                        nc.vector.tensor_tensor(out=ysum[:, c, :], in0=m2[:, 0:DI], in1=ysum[:, c, :],
                                                op=ALU.add).then_inc(y_taken, 1)
                        wait(vec, y_taken, b, C, c + 1)
                        link(nc.vector.tensor_tensor(out=ysum[:, c, :], in0=ysum[:, c, :], in1=xskip[:, c, :], op=ALU.add))
                    wait(vec, z_ready, b, 2, c // 2 + 1)
                    nc.vector.tensor_tensor(out=y[:, c, :], in0=ysum[:, c, :], in1=zs[:, c, :],
                                            op=ALU.mult).then_inc(y_ready, 1)

                def hidden(u):
                    e, f = u // FT, u % FT
                    wait(vec, sg_ready, q, U, u + 1)
                    wait(vec, ev_psum, q, U, u + 1)
                    if f == 0 and e >= 2:
                        wait(vec, o_psum, q, E, e - 1)
                    nc.vector.scalar_tensor_tensor(out=hid[:, e % 2, f, :], in0=pv[u % 2][:, :], scalar=b12[:, 2 * u + 1:2 * u + 2],
                                                   in1=sg[:, u % 2, :], op0=ALU.add, op1=ALU.mult).then_inc(hid_ready, 1)

                def split_first_input(n):
                    wait(vec, h_ready, n, 1, 1)
                    nc.vector.tensor_copy(h_hi[:, :], h[:, :]).then_inc(hhi_ready, 1)
                    wait(vec, hhi_ready, n, 1, 1)
                    nc.vector.tensor_tensor(out=h_lo[:, :], in0=h[:, :], in1=h_hi[:, :].bitcast(F32),
                                            op=ALU.subtract).then_inc(hlo_ready, 1)

                def softplus_exponent():
                    wait(vec, dt_psum, b, 1, 1)
                    nc.vector.tensor_tensor(out=raw[:, :], in0=m1[:, 0:C * NH], in1=dt_bias, op=ALU.add).then_inc(dt_taken, 1)
                    wait(vec, dt_taken, b, 1, 1)
                    nc.vector.scalar_tensor_tensor(out=neg_abs[:, :], in0=raw[:, :], scalar=-1.0, in1=raw[:, :],
                                                   op0=ALU.mult, op1=ALU.min).then_inc(neg_abs_ready, 1)

                def softplus_rest():
                    wait(vec, exp_neg_ready, b, 1, 1)
                    link(nc.vector.tensor_scalar(two_plus[:, :], exp_neg[:, :], 2.0, None, ALU.add))
                    link(nc.vector.reciprocal(inverse[:, :], two_plus[:, :]))
                    link(nc.vector.tensor_tensor(out=arg[:, :], in0=exp_neg[:, :], in1=inverse[:, :], op=ALU.mult))
                    link(nc.vector.tensor_tensor(out=arg_sq[:, :], in0=arg[:, :], in1=arg[:, :], op=ALU.mult))
                    link(nc.vector.tensor_scalar(series[:, :], arg_sq[:, :], 1.0 / LAST, None, ALU.mult))
                    for k in range(LAST - 2, 2, -2):
                        link(nc.vector.scalar_tensor_tensor(out=series[:, :], in0=series[:, :], scalar=1.0 / k, in1=arg_sq[:, :],
                                                            op0=ALU.add, op1=ALU.mult))
                    nc.vector.tensor_scalar(raw_pos[:, :], raw[:, :], 0.0, None, ALU.max)
                    link(nc.vector.scalar_tensor_tensor(out=series[:, :], in0=series[:, :], scalar=1.0, in1=arg[:, :],
                                                        op0=ALU.add, op1=ALU.mult))
                    link(nc.vector.scalar_tensor_tensor(out=dt[:, :], in0=series[:, :], scalar=2.0, in1=raw_pos[:, :],
                                                        op0=ALU.mult, op1=ALU.add))
                    link(nc.vector.tensor_tensor(out=da[:, :], in0=dt[:, :], in1=nega[:, :], op=ALU.mult))
                    link(nc.vector.tensor_copy(da_hi[:, :], da[:, :]))
                    nc.vector.tensor_tensor(out=da_lo[:, :], in0=da[:, :], in1=da_hi[:, :].bitcast(F32),
                                            op=ALU.subtract).then_inc(da_ready, 1)

                def x1_and_norm():
                    wait(vec, rstdy_ready, b, 1, 1)
                    wait(vec, out_psum, b, 1, 1)
                    wait(vec, xo_ready, b, 1, -1)
                    for c in range(C):
                        last = nc.vector.scalar_tensor_tensor(out=x1[:, par, c, :], in0=m1[:, c * D:(c + 1) * D],
                                                              scalar=rstdy[:, c:c + 1], in1=x[:, par, c, :],
                                                              op0=ALU.mult, op1=ALU.add)
                    last.then_inc(x1_ready, 1)
                    wait(vec, x1_ready, b, 1, 1)
                    norm(x1[:, par, :, :], mv, var, norm2_var)

                if isinstance(b, int) and b == 0:
                    vec.wait_ge(x_in, 16)
                    norm(x[:, 0, :, :], next_mv, next_var, norm1_var)
                    set_up()
                    vec.wait_ge(const_ready, 1)
                    norm_end(next_xn, x[:, 0, :, :], next_mv, next_rstd, norm1_rstd, 0, norm1_ready)
                    all_gates()
                    split_first_input(0)
                else:
                    count[0] = 2
                if isinstance(b, int) and b == 1:
                    vec.wait_ge(w12_lo_ready, U)
                for u in range(U):
                    if b is not None and u in (2, 5):
                        conv_taps(0 if u == 2 else 3)
                    if b is not None and u == 7:
                        wait(vec, g_psum, b, 1, 1)
                        nc.vector.tensor_tensor(out=gm[:, :, :], in0=m2[:, :].rearrange("p (c t) -> p c t", c=C),
                                                in1=upto[:, :].unsqueeze(1).to_broadcast([P, C, P]),
                                                op=ALU.mult).then_inc(gm_ready, 1)
                        wait(vec, gm_ready, b, 1, 1)
                    if b is not None and u == 13:
                        x1_and_norm()
                    if b is not None and u == 7:
                        mix_chunk(0)
                        for c in (2, 3):
                            wait(vec, tok_psum, b, C, c + 1)
                            nc.vector.tensor_copy(tok[:, c, :], tok_bank[c % 2][:, 0:DI + P]).then_inc(late_tok_ready, 1)
                    if q is not None:
                        hidden(u)
                    if b is None:
                        continue
                    if u == 1:
                        softplus_exponent()
                    if u == 2:
                        softplus_rest()
                    if u == 13:
                        norm_end(xn, x1[:, par, :, :], mv, rstd, norm2_rstd, b, norm2_ready)
                    if 3 <= u < 5:
                        conv_taps(u - 2)
                    if u == 6:
                        wait(vec, gate_in, b, 16, 16)
                        nc.vector.tensor_tensor(out=wo[:, :, :], in0=woutn[:, :, :],
                                                in1=gate[:, par, 0:D].unsqueeze(1).to_broadcast([P, 2, D]),
                                                op=ALU.mult).then_inc(wo_ready, 1)
                    if u == 13 and not (isinstance(b, int) and b == B - 1):
                        norm_end(next_xn, x[:, 1 - par, :, :], next_mv, next_rstd, norm1_rstd, b + 1, norm1_ready)
                    if 8 <= u < 7 + C:
                        mix_chunk(u - 7)
                    if 8 <= u < 7 + C:
                        c = u - 8
                        if c == 0:
                            wait(vec, snew_psum, b, C - 1, c + 1)
                            nc.vector.tensor_copy(state[:, 0, :], m1[:, 0:DI]).then_inc(state_ready, 1)
                        else:
                            wait(vec, state_ready, b, C - 1, c)
                            link(nc.vector.tensor_tensor(out=faded[:, c, :].rearrange("p (h d) -> p h d", h=NH),
                                                         in0=state[:, c - 1, :].rearrange("p (h d) -> p h d", h=NH),
                                                         in1=wide(edge[:, 1, c, :], HD), op=ALU.mult))
                            wait(vec, snew_psum, b, C - 1, c + 1)
                            nc.vector.tensor_tensor(out=state[:, c, :], in0=m1[:, 0:DI], in1=faded[:, c, :],
                                                    op=ALU.add).then_inc(state_ready, 1)
                    if 8 <= u < 8 + C:
                        y_chunk(u - 8)
                    if u == 12:
                        wait(vec, sq_ready, b, C, C)
                        nc.vector.tensor_scalar(ms[:, :], ss[:, :], 1.0 / DI, EPS, ALU.mult, ALU.add).then_inc(ms_ready, 1)
                    if u == 12 and not (isinstance(b, int) and b == B - 1):
                        wait(vec, x_in, b, 16, 32)
                        norm(x[:, 1 - par, :, :], next_mv, next_var, norm1_var)
                    if u == 15:
                        wait(vec, h2_ready, b, 1, 1)
                        nc.vector.tensor_copy(h2_hi[:, par, :], h2[:, :]).then_inc(h2hi_ready, 1)
                if b is not None:
                    wait(vec, route_psum, b, 1, 1)
                    link(nc.vector.tensor_copy(logit[:, :, :].rearrange("p c e -> p (c e)"), m1[:, 0:C * E]))
                    nc.vector.tensor_copy(touch[:, 1:2], logit[:, 0, 0:1])
                    for c in range(C):
                        last = nc.vector.max(top[:, c, :], logit[:, c, :])
                    link(last)
                    nc.vector.tensor_tensor(out=gap[:, :], in0=top[:, :, 0], in1=top[:, :, 1], op=ALU.subtract).then_inc(gap_ready, 1)
                    for c in range(C):
                        last = nc.vector.max_index(topi[:, c, :], top[:, c, :], logit[:, c, :])
                    link(last)
                    link(nc.vector.tensor_copy(topf[:, :, :], topi[:, :, 0:2]))
                    wait(vec, tanh_ready, b, 1, 1)
                    nc.vector.tensor_scalar(wtop[:, :, 0], tanh[:, :], 0.5, 0.5, ALU.mult, ALU.add)
                    link(nc.vector.tensor_scalar(wtop[:, :, 1], tanh[:, :], -0.5, 0.5, ALU.mult, ALU.add))
                    for c in range(C):
                        last = nc.vector.tensor_scalar(pick[:, c, :], experts[:, :], topf[:, c, 0:1], wtop[:, c, 0:1],
                                                       ALU.is_equal, ALU.mult)
                    for c in range(C):
                        last = nc.vector.tensor_scalar(comb[:, par, c, :], experts[:, :], topf[:, c, 1:2], wtop[:, c, 1:2],
                                                       ALU.is_equal, ALU.mult)
                    link(last)
                    nc.vector.tensor_tensor(out=comb[:, par, :, :], in0=comb[:, par, :, :], in1=pick[:, :, :],
                                            op=ALU.add).then_inc(comb_ready, 1)
                    if not (isinstance(b, int) and b == B - 1):
                        split_first_input(b + 1)
                    assert count[0] == STEPS + (0 if isinstance(b, int) and b == B - 1 else 2), (b, count[0])

            run(vec, steps)

        @block.tensor
        def _(pe):
            def split_mm(out, w, m, start=True, stop=True):
                nc.tensor.matmul(out, w[1], m[0], start=start, stop=False)
                nc.tensor.matmul(out, w[0], m[1], start=False, stop=False)
                return nc.tensor.matmul(out, w[0], m[0], start=False, stop=stop)

            pe.wait_ge(s_cs, 1)
            for r in (SA, CA, SB, CB):
                last = nc.tensor.matmul(m0[:, r * B:(r + 1) * B], wmod[:, r, :], cs[:, :], start=True, stop=True)
            last.then_inc(s_mod, 1)
            for k, r in ((0, GA), (1, GB)):
                last = nc.tensor.matmul(m2[0:B, k * D:(k + 1) * D], cs[:, :], wmod[:, r, :], start=True, stop=True)
            last.then_inc(gate_psum, 1)
            pe.wait_ge(s_modt, 1)
            pe.wait_ge(const_ready, 1)

            def steps(b, par, q):
                def turn_first(n):
                    wait(pe, norm1_ready, n, 1, 1)
                    wait(pe, h2_ready, n, 1)
                    for c in range(C):
                        last = nc.tensor.transpose(m0[:, c * P:(c + 1) * P], next_xn[:, c, :], ident[:, :])
                    last.then_inc(ht_psum, 1)

                def project_in(i):
                    if i == 1:
                        wait(pe, dt_taken, b, 1, 1)
                    if i == 2:
                        wait(pe, tapped, b, NCT, 1)
                    if i == 3:
                        wait(pe, z_ready, b, 2, 2)
                    o = DI + i * P
                    split_mm(in_bank[i][:, :], (win_hi[:, o:o + P], win_lo[:, o:o + P]),
                             (h_hi[:, :], h_lo[:, :])).then_inc(in_psum, 1)

                def project_z(k):
                    if k == 0:
                        wait(pe, y_taken, b, C)
                        if isinstance(b, int) and b == 0:
                            pe.wait_ge(gate_step, 2)
                    else:
                        wait(pe, z_ready, b, 2, 1)
                    for n in range(2):
                        t = slice((2 * k + n) * P, (2 * k + n + 1) * P)
                        last = split_mm(m2[:, n * DI:(n + 1) * DI], (h_hi[:, t], h_lo[:, t]), (win_hi[:, 0:DI], win_lo[:, 0:DI]))
                    last.then_inc(z_psum, 1)

                def segments(c):
                    wait(pe, mda_ready, b, C, c + 1)
                    if c < 3:
                        wait(pe, tapped, b, NCT, c + 2)
                    else:
                        wait(pe, decayed, b, C, 1)
                    o = seg_bank[c][:, :]
                    nc.tensor.matmul(o, after_r[:, :], mda_lo[:, c % 2, :, :].rearrange("p h t -> p (h t)"), start=True, stop=False)
                    nc.tensor.matmul(o, after_r[:, :], mda_hi[:, c % 2, :, :].rearrange("p h t -> p (h t)"), start=False,
                                     stop=True).then_inc(seg_psum, 1)

                def to_tokens(c):
                    if c == 0:
                        wait(pe, silued, b, NCT, NCT)
                        wait(pe, edge_ready, b, 1, 1)
                    elif c == 1:
                        wait(pe, decayed, b, C, C)
                    else:
                        wait(pe, tok_ready, b, 2, c - 1)
                    for i in range(3):
                        last = nc.tensor.transpose(tok_bank[c % 2][:, i * P:(i + 1) * P], xbc[:, i, c * P:(c + 1) * P], ident[:, :])
                    last.then_inc(tok_psum, 1)

                def turn_last_tokens():
                    to_tokens(2)
                    to_tokens(3)

                def new_state(c):
                    wait(pe, xdecay_ready, b, C - 1, c + 1)
                    if c == 0:
                        wait(pe, late_tok_ready, b, 2, 2)
                    else:
                        wait(pe, state_ready, b, C - 1, c)
                    nc.tensor.matmul(m1[:, 0:DI], tok[:, c, DI:DI + P], xdecay[:, c, :], start=True, stop=True).then_inc(snew_psum, 1)

                def outputs(c):
                    wait(pe, mixed, b, C, c + 1)
                    wait(pe, xdt_ready, b, C, c + 1)
                    if c == 0:
                        wait(pe, gm_ready, b, 1, 1)
                    else:
                        wait(pe, y_taken, b, C, c)
                    for n in range(NH):
                        last = nc.tensor.matmul(m2[:, n * HD:(n + 1) * HD], mix[:, c, n, :], xdt[:, c, n * HD:(n + 1) * HD],
                                                start=True, stop=True)
                    if c > 0:
                        wait(pe, state_ready, b, C - 1, c)
                        last = nc.tensor.matmul(m2[:, DI:2 * DI], xbc[:, 3, c * P:(c + 1) * P], state[:, c - 1, :],
                                                start=True, stop=True)
                    last.then_inc(y_psum, 1)

                def turn_y(c):
                    wait(pe, y_ready, b, C, c + 1)
                    wait(pe, late_tok_ready, b, 2, 2)
                    if c > 0:
                        wait(pe, yt_ready, b, C, c)
                    for k in range(2):
                        last = nc.tensor.transpose(m0[:, k * P:(k + 1) * P], y[:, c, k * P:(k + 1) * P], ident[:, :])
                    last.then_inc(yt_psum, 1)

                def up(u, between=None):
                    if u == 0:
                        wait(pe, h2hi_ready, q, 1, 1)
                        wait(pe, h2lo_ready, q, 1, 1)
                    if u >= 2:
                        wait(pe, hid_ready, q, U, u - 1)
                    p2 = 1 - par
                    for k, o, s in ((0, pg, eg_psum), (1, pv, ev_psum)):
                        if k == 1 and between is not None:
                            between()
                        w = slice((2 * u + k) * P, (2 * u + k + 1) * P)
                        split_mm(o[u % 2][:, :], (w12_hi[:, w], w12_lo[:, w]), (h2_hi[:, p2, :], h2_lo[:, p2, :])).then_inc(s, 1)

                def down(e):
                    wait(pe, hid_ready, q, U, FT * (e + 1))
                    if e == 0:
                        wait(pe, acc_started, q, 1, 1)
                    else:
                        wait(pe, eo_ready, q, E, e)
                    for c in range(C):
                        for f in range(FT):
                            last = nc.tensor.matmul(po[:, c * D:(c + 1) * D], hid[:, e % 2, f, c * P:(c + 1) * P],
                                                    w3[:, FT * e + f, :], start=(f == 0), stop=(f == FT - 1))
                    last.then_inc(o_psum, 1)

                if isinstance(b, int) and b == 0:
                    turn_first(0)
                for u in range(U):
                    if q is not None:
                        up(u, turn_last_tokens if u == 8 and b is not None else None)
                    elif u == 8:
                        turn_last_tokens()
                    if b is not None and u == 15:
                        wait(pe, norm2_ready, b, 1, 1)
                        wait(pe, yt_ready, b, C, C)
                        for c in range(C):
                            last = nc.tensor.transpose(m0[:, c * P:(c + 1) * P], xn[:, c, :], ident[:, :])
                        last.then_inc(h2t_psum, 1)
                    if q is not None:
                        if u == 1:
                            wait(pe, comb_ready, q, 1, 1)
                            wait(pe, eo_ready, q, E)
                            for c in range(C):
                                last = nc.tensor.transpose(po[0:E, c * P:(c + 1) * P], comb[:, 1 - par, c, :], ident[:, :])
                            last.then_inc(combt_psum, 1)
                        if u == 2:
                            wait(pe, combt_ready, q, 1, 1)
                            for c in range(C):
                                last = nc.tensor.matmul(po[:, c * D:(c + 1) * D], combt[:, c * P:(c + 1) * P], b3[:, :], start=True,
                                                        stop=True)
                            last.then_inc(b3_psum, 1)
                        if u >= 3 and u % 2 == 1:
                            down(u // 2 - 1)
                    if b is None:
                        continue
                    if u == 1:
                        wait(pe, hhi_ready, b, 1, 1)
                        wait(pe, hlo_ready, b, 1, 1)
                        wait(pe, gap_ready, b, 1)
                        for c in range(C):
                            t = slice(c * P, (c + 1) * P)
                            last = split_mm(m1[:, c * NH:(c + 1) * NH], (h_hi[:, t], h_lo[:, t]), (win_hi[:, NIN - NH:], win_lo[:, NIN - NH:]))
                        last.then_inc(dt_psum, 1)
                        project_in(0)
                    if u == 2:
                        project_in(1)
                        project_z(0)
                    if u == 3:
                        project_in(2)
                        project_z(1)
                    if u == 4:
                        project_in(3)
                    if u == 5:
                        segments(0)
                        segments(1)
                    if u == 6:
                        segments(2)
                    if u == 7:
                        segments(3)
                        wait(pe, decayed, b, C, 2)
                        for k, w in enumerate((upto_r, ones_r)):
                            o = m0[:, k * C * NH:(k + 1) * C * NH]
                            nc.tensor.matmul(o, w[:, :], da_lo[:, :], start=True, stop=False)
                            last = nc.tensor.matmul(o, w[:, :], da_hi[:, :], start=False, stop=True)
                        last.then_inc(edge_psum, 1)
                        wait(pe, decayed, b, C, 3)
                        wait(pe, silued, b, NCT, NCT)
                        for c in range(C):
                            t = slice(c * P, (c + 1) * P)
                            last = nc.tensor.matmul(m2[:, t], xbc[:, 2, t], xbc[:, 3, t], start=True, stop=True)
                        last.then_inc(g_psum, 1)
                        to_tokens(0)
                        to_tokens(1)
                    if 9 <= u < 7 + C:
                        new_state(u - 8)
                    if 8 <= u < 8 + C:
                        outputs(u - 8)
                    if u == 8:
                        new_state(0)
                    if 9 <= u < 8 + C:
                        turn_y(u - 9)
                    if u == 12:
                        wait(pe, wo_ready, b, 1, 1)
                        wait(pe, state_ready, b, C - 1, C - 1)
                        for c in range(C):
                            if c == 1:
                                turn_y(C - 1)
                            if c in (0, C - 1):
                                wait(pe, yt_ready, b, C, C - 1 if c == 0 else C)
                            for k in range(2):
                                last = nc.tensor.matmul(m1[:, c * D:(c + 1) * D], yt[:, c, k, :], wo[:, k, :], start=(k == 0),
                                                        stop=(k == 1))
                        last.then_inc(out_psum, 1)
                    if u == 15:
                        wait(pe, h2_ready, b, 1, 1)
                        for c in range(C):
                            last = nc.tensor.matmul(m1[:, c * E:(c + 1) * E], h2[:, c * P:(c + 1) * P], wg[:, :], start=True, stop=True)
                        last.then_inc(route_psum, 1)
                        if not (isinstance(b, int) and b == B - 1):
                            turn_first(b + 1)
                if q is not None:
                    down(E - 1)
                if isinstance(b, int) and b == 0:
                    pe.wait_ge(w12_hi_ready, U)
                    pe.wait_ge(w12_lo_ready, U)
                    pe.wait_ge(w3_in, 16)

            run(pe, steps)


def kernel(**inputs):
    import numpy as np
    import concourse.bacc as bacc
    from concourse.bass_utils import run_bass_kernel_spmd as launch

    g = {k.replace("L0_attn_", "").replace("L0_ffn_", "f_").replace("L0_", ""): np.asarray(v) for k, v in inputs.items()}
    arr = np.ascontiguousarray
    to = lambda v, n: np.broadcast_to(v, (n,) + v.shape)
    part = {
        "ident": np.eye(P, dtype=np.float32),
        "upto": np.triu(np.ones((P, P), np.float32)),
        "after": np.tril(np.ones((P, P), np.float32), -1),
        "expo": np.full((P, C), -0.5, np.float32),
        "experts": to(np.arange(E, dtype=np.float32), P),
        "conv_w": g["conv_w"].reshape(NCT, P, KC).transpose(1, 0, 2).reshape(P, NCT * KC),
        "conv_b": g["conv_b"].reshape(NCT, P).T,
        "b12": np.stack([g["f_b1"].reshape(U, P), g["f_b2"].reshape(U, P)], 1).reshape(2 * U, P).T,
        "norm_w": g["norm_w"].reshape(2, P).T,
        "dt_bias": to(np.tile(g["dt_bias"], C), P),
        "a_log": to(np.tile(g["A_log"], C), P),
        "d_row": to(np.repeat(g["D"], HD), P),
        "ct": g["c"].T,
        "wg": g["f_Wg"].T,
    }
    data = {
        "x": g["X"],
        "win": arr(g["W_in"].T),
        "wout": arr(g["W_out"].T.reshape(2, P, D).transpose(1, 0, 2)),
        "w12": arr(np.stack([g["f_W1"].reshape(U, P, D), g["f_W2"].reshape(U, P, D)], 1).reshape(2 * U * P, D).T),
        "w3": arr(g["f_W3"].transpose(0, 2, 1).reshape(U, P, D).transpose(1, 0, 2)),
        "b3": g["f_b3"],
        "wmod": arr(g["wmod"].reshape(D, 6, D)),
        "table": np.concatenate([part[name] for name, _ in TABLE], axis=1),
    }
    nc = bacc.Bacc("TRN2", target_bir_lowering=False, num_devices=1)
    aps = {k: nc.dram_tensor(f"in_{k}", v.shape, mybir.dt.from_np(v.dtype), kind="ExternalInput").ap() for k, v in data.items()}
    aps["gates"] = nc.dram_tensor("gates", (B, 2 * D), F32, kind="Internal").ap()
    aps["out"] = nc.dram_tensor("out", (B, L, D), F32, kind="ExternalOutput").ap()
    program(nc, aps)
    r = launch(nc, [{f"in_{k}": v for k, v in data.items()}], core_ids=[0])
    return r.results[0]["out"]
```
